# Optimizing a Trainium2 kernel written in Bass

```python
import numpy as np
import jax
import jax.numpy as jnp

def _softmax(x, axis=-1):
    return jax.nn.softmax(x, axis=axis)

def _gelu(x):
    return jax.nn.gelu(x, approximate=True)

def _silu(x):
    return jax.nn.silu(x)

def _sigmoid(x):
    return jax.nn.sigmoid(x)

def _layernorm(x, axis=-1, eps=1e-05):
    m = jnp.mean(x, axis=axis, keepdims=True)
    v = jnp.var(x, axis=axis, keepdims=True)
    return (x - m) / jnp.sqrt(v + eps)

def _scatter_add(tgt, idx, src, axis=0):
    return tgt.at[idx].add(src)

def _segment_sum(src, seg, n):
    return jax.ops.segment_sum(src, seg, n)
kernel_name = 'mk_decoder_postln_d1_seqx_r8_8c92fd'

def setup_inputs(seed: int=0):
    np.random.seed(seed)
    _w = jnp.asarray

    def _rec_inputs():
        import jax
        import jax.numpy as jnp
        _rk = jax.random.key(seed)
        x = 0.0001212 + 1 * jax.random.normal(jax.random.fold_in(_rk, 1), (8, 128, 256), jnp.float32)
        _lenS = 128 - jax.random.randint(jax.random.fold_in(_rk, 7), (8,), 0, max(1, 128 // 4) + 1, jnp.int32)
        _lenS2 = 128 - jax.random.randint(jax.random.fold_in(_rk, 8), (8,), 0, max(1, 128 // 4) + 1, jnp.int32)
        _ctx_2048P = jax.random.normal(jax.random.fold_in(_rk, 11), (8, 16, 256), jnp.float32)
        _ctx_2048c = jax.random.dirichlet(jax.random.fold_in(_rk, 511), 0.3 * jnp.ones((16,), jnp.float32), (8, 128))
        _ctx_2048t = jnp.einsum('bsk,bkd->bsd', _ctx_2048c, _ctx_2048P)
        _ctx_2048t = _ctx_2048t * jax.lax.rsqrt(jnp.mean(jnp.square(_ctx_2048t)) + 1e-12) * 0.953939
        ctx_2048 = 0.000173663 + 1.0001 * (_ctx_2048t + 0.3 * jax.random.normal(jax.random.fold_in(_rk, 611), (8, 128, 256), jnp.float32))
        return (x, ctx_2048)
    x, ctx_2048 = _rec_inputs()

    def _L0_attn_setup():
        import jax, jax.numpy as jnp
        import numpy as np
        B, T, D = (4, 512, 256)
        W_SCALE = 0.02
        key = jax.random.key(seed)
        ks = jax.random.split(key, 10)
        x = jax.random.normal(ks[0], (B, T, D), dtype=jnp.float32)
        Wk = jax.random.normal(ks[1], (D, D), dtype=jnp.float32) * W_SCALE
        Wv = jax.random.normal(ks[2], (D, D), dtype=jnp.float32) * W_SCALE
        Wr = jax.random.normal(ks[3], (D, D), dtype=jnp.float32) * W_SCALE
        Wo = jax.random.normal(ks[4], (D, D), dtype=jnp.float32) * W_SCALE
        bk = jnp.zeros((D,), jnp.float32)
        bv = jnp.zeros((D,), jnp.float32)
        br = jnp.zeros((D,), jnp.float32)
        bo = jnp.zeros((D,), jnp.float32)
        tmk = jax.random.uniform(ks[5], (D,), dtype=jnp.float32)
        tmv = jax.random.uniform(ks[6], (D,), dtype=jnp.float32)
        tmr = jax.random.uniform(ks[7], (D,), dtype=jnp.float32)
        u = jax.random.normal(ks[8], (D,), dtype=jnp.float32) * 0.1
        w = jax.random.uniform(ks[9], (D,), dtype=jnp.float32)
        return {'x': x, 'Wk': Wk, 'bk': bk, 'Wv': Wv, 'bv': bv, 'Wr': Wr, 'br': br, 'Wo': Wo, 'bo': bo, 'tmk': tmk, 'tmv': tmv, 'tmr': tmr, 'u': u, 'w': w}
    _L0_attn_all = _L0_attn_setup()
    _L0_attn_in = {k: v for k, v in _L0_attn_all.items() if k in ('Wk', 'bk', 'Wv', 'bv', 'Wr', 'br', 'Wo', 'bo', 'tmk', 'tmv', 'tmr', 'u', 'w')}
    del _L0_attn_all

    def _L0_xattn_setup():
        import jax, jax.numpy as jnp
        import numpy as np
        B_DIM, T_DIM, C_DIM = (16, 128, 256)

        def _wkv(w, u, k, v):
            Bn, Tn, Cn = k.shape
            NEG_INF = jnp.float32(-1e+38)

            def step(carry, kv_t):
                p, q, o = carry
                kt, vt = kv_t
                no = jnp.maximum(o, u + kt)
                A = jnp.exp(o - no)
                E = jnp.exp(u + kt - no)
                y = (A * p + E * vt) / (A * q + E)
                no2 = jnp.maximum(w + o, kt)
                A2 = jnp.exp(w + o - no2)
                E2 = jnp.exp(kt - no2)
                return ((A2 * p + E2 * vt, A2 * q + E2, no2), y)
            init = (jnp.zeros((Bn, Cn), k.dtype), jnp.zeros((Bn, Cn), k.dtype), jnp.full((Bn, Cn), NEG_INF, k.dtype))
            kT = jnp.moveaxis(k, 1, 0)
            vT = jnp.moveaxis(v, 1, 0)
            _, yT = jax.lax.scan(step, init, (kT, vT))
            return jnp.moveaxis(yT, 0, 1)
        key = jax.random.key(seed)
        k1, k2, k3, k4 = jax.random.split(key, 4)
        w = -jnp.exp(jax.random.normal(k1, (C_DIM,), jnp.float32))
        u = jax.random.normal(k2, (C_DIM,), jnp.float32)
        k = jax.random.normal(k3, (B_DIM, T_DIM, C_DIM), jnp.float32)
        v = jax.random.normal(k4, (B_DIM, T_DIM, C_DIM), jnp.float32)
        return {'B': B_DIM, 'T': T_DIM, 'C': C_DIM, 'w': w, 'u': u, 'k': k, 'v': v}
    _L0_xattn_all = _L0_xattn_setup()
    _L0_xattn_in = {k: v for k, v in _L0_xattn_all.items() if k in ('w', 'u')}
    del _L0_xattn_all

    def _L0_ffn_setup():
        import jax, jax.numpy as jnp
        import numpy as np
        B, S, H, E, K, I = (2, 128, 256, 32, 8, 96)
        key = jax.random.key(seed)
        ks = jax.random.split(key, 5)
        scaled = lambda k, shp, fan: jax.random.normal(k, shp, jnp.float32) * fan ** (-0.5)
        return {'hidden_states': jax.random.normal(ks[0], (B, S, H), jnp.float32), 'router_w': scaled(ks[1], (E, H), H), 'w_gate': scaled(ks[2], (E, H, I), H), 'w_up': scaled(ks[3], (E, H, I), H), 'w_down': scaled(ks[4], (E, I, H), I)}
    _L0_ffn_all = _L0_ffn_setup()
    _L0_ffn_in = {k: v for k, v in _L0_ffn_all.items() if k in ('router_w', 'w_gate', 'w_up', 'w_down')}
    del _L0_ffn_all
    return {'x': x, 'ctx_2048': ctx_2048, 'L0_attn_Wk': _L0_attn_in['Wk'], 'L0_attn_bk': _L0_attn_in['bk'], 'L0_attn_Wv': _L0_attn_in['Wv'], 'L0_attn_bv': _L0_attn_in['bv'], 'L0_attn_Wr': _L0_attn_in['Wr'], 'L0_attn_br': _L0_attn_in['br'], 'L0_attn_Wo': _L0_attn_in['Wo'], 'L0_attn_bo': _L0_attn_in['bo'], 'L0_attn_tmk': _L0_attn_in['tmk'], 'L0_attn_tmv': _L0_attn_in['tmv'], 'L0_attn_tmr': _L0_attn_in['tmr'], 'L0_attn_u': _L0_attn_in['u'], 'L0_attn_w': _L0_attn_in['w'], 'L0_xattn_w': _L0_xattn_in['w'], 'L0_xattn_u': _L0_xattn_in['u'], 'L0_ffn_router_w': _L0_ffn_in['router_w'], 'L0_ffn_w_gate': _L0_ffn_in['w_gate'], 'L0_ffn_w_up': _L0_ffn_in['w_up'], 'L0_ffn_w_down': _L0_ffn_in['w_down']}

def reference(x, ctx_2048, L0_attn_Wk, L0_attn_bk, L0_attn_Wv, L0_attn_bv, L0_attn_Wr, L0_attn_br, L0_attn_Wo, L0_attn_bo, L0_attn_tmk, L0_attn_tmv, L0_attn_tmr, L0_attn_u, L0_attn_w, L0_xattn_w, L0_xattn_u, L0_ffn_router_w, L0_ffn_w_gate, L0_ffn_w_up, L0_ffn_w_down):
    import jax
    import jax.numpy as jnp

    def _L0_attn_ref(x, Wk, bk, Wv, bv, Wr, br, Wo, bo, tmk, tmv, tmr, u, w):
        import jax, jax.numpy as jnp
        import numpy as np
        B, T, D = (4, 512, 256)
        W_SCALE = 0.02
        xs = jnp.pad(x, ((0, 0), (1, 0), (0, 0)))[:, :-1]
        k = x * tmk + xs * (1.0 - tmk)
        v = x * tmv + xs * (1.0 - tmv)
        r = jax.nn.silu(x * tmr + xs * (1.0 - tmr))
        k = jnp.einsum('btd,ed->bte', k, Wk) + bk
        v = jnp.einsum('btd,ed->bte', v, Wv) + bv
        r = jnp.einsum('btd,ed->bte', r, Wr) + br

        def step(carry, kv_t):
            a, b = carry
            k_t, v_t = kv_t
            t = jnp.maximum(u + k_t, w)
            e1 = jnp.exp(-w - t)
            e2 = jnp.exp(u + k_t - t)
            a = e1 * a + e2 * v_t
            b = e1 * b + e2
            return ((a, b), a / b)
        a0 = jnp.zeros((x.shape[0], x.shape[2]), x.dtype)
        b0 = jnp.zeros_like(a0)
        _, wkv = jax.lax.scan(step, (a0, b0), (k.transpose(1, 0, 2), v.transpose(1, 0, 2)))
        wkv = wkv.transpose(1, 0, 2)
        return jnp.einsum('btd,ed->bte', wkv * r, Wo) + bo

    def _L0_xattn_ref(B, T, C, w, u, k, v):
        import jax, jax.numpy as jnp
        import numpy as np
        B_DIM, T_DIM, C_DIM = (16, 128, 256)

        def _wkv(w, u, k, v):
            Bn, Tn, Cn = k.shape
            NEG_INF = jnp.float32(-1e+38)

            def step(carry, kv_t):
                p, q, o = carry
                kt, vt = kv_t
                no = jnp.maximum(o, u + kt)
                A = jnp.exp(o - no)
                E = jnp.exp(u + kt - no)
                y = (A * p + E * vt) / (A * q + E)
                no2 = jnp.maximum(w + o, kt)
                A2 = jnp.exp(w + o - no2)
                E2 = jnp.exp(kt - no2)
                return ((A2 * p + E2 * vt, A2 * q + E2, no2), y)
            init = (jnp.zeros((Bn, Cn), k.dtype), jnp.zeros((Bn, Cn), k.dtype), jnp.full((Bn, Cn), NEG_INF, k.dtype))
            kT = jnp.moveaxis(k, 1, 0)
            vT = jnp.moveaxis(v, 1, 0)
            _, yT = jax.lax.scan(step, init, (kT, vT))
            return jnp.moveaxis(yT, 0, 1)
        return _wkv(w, u, k, v)

    def _L0_ffn_ref(hidden_states, router_w, w_gate, w_up, w_down):
        import jax, jax.numpy as jnp
        import numpy as np
        B, S, H, E, K, I = (2, 128, 256, 32, 8, 96)
        Bq, Sq, Hd = hidden_states.shape
        x = hidden_states.reshape(-1, Hd)
        logits = x @ router_w.T
        probs = jax.nn.softmax(logits.astype(jnp.float32), axis=-1)
        rw, sel = jax.lax.top_k(probs, K)
        rw = rw / jnp.sum(rw, axis=-1, keepdims=True)
        rw = rw.astype(x.dtype)

        def body(acc, operand):
            e, wg, wu, wd = operand
            w_e = jnp.sum(jnp.where(sel == e, rw, jnp.zeros_like(rw)), axis=-1)
            h = jax.nn.silu(x @ wg) * (x @ wu)
            return (acc + h @ wd * w_e[:, None], None)
        acc0 = jnp.zeros_like(x)
        acc, _ = jax.lax.scan(body, acc0, (jnp.arange(E), w_gate, w_up, w_down))
        return acc.reshape(Bq, Sq, Hd)
    x = _layernorm(x + _L0_attn_ref(x, L0_attn_Wk, L0_attn_bk, L0_attn_Wv, L0_attn_bv, L0_attn_Wr, L0_attn_br, L0_attn_Wo, L0_attn_bo, L0_attn_tmk, L0_attn_tmv, L0_attn_tmr, L0_attn_u, L0_attn_w), axis=-1)
    x = _layernorm(x + _L0_xattn_ref(8, 128, 256, L0_xattn_w, L0_xattn_u, x, ctx_2048), axis=-1)
    x = _layernorm(x + _L0_ffn_ref(x, L0_ffn_router_w, L0_ffn_w_gate, L0_ffn_w_up, L0_ffn_w_down), axis=-1)
    return x

_drawn_inputs = setup_inputs


def setup_inputs(seed=0):
    import zlib

    import numpy as np

    out = dict(_drawn_inputs(seed))
    spreads = {'L0_attn_bk': (0.0, 0.8),
     'L0_attn_bv': (0.0, 0.8),
     'L0_attn_br': (0.0, 0.756),
     'L0_attn_bo': (0.0, 2.0)}
    factors = {'L0_attn_Wk': 8.0,
     'L0_attn_Wv': 3.983,
     'L0_attn_Wr': 4.259,
     'L0_attn_Wo': 3.815,
     'L0_attn_tmk': 8.0,
     'L0_attn_tmv': 8.0,
     'L0_attn_tmr': 7.328,
     'L0_attn_u': 8.0,
     'L0_attn_w': 8.0}
    for name, (base, spread) in spreads.items():
        noise = np.random.default_rng([zlib.crc32(name.encode()), seed]).standard_normal(out[name].shape)
        drawn = base * np.exp(spread * noise) if base else spread * noise
        out[name] = jnp.asarray(drawn.astype(out[name].dtype))
    for name, factor in factors.items():
        out[name] = (out[name] * factor).astype(out[name].dtype)
    return out
```

```python
import concourse.bass as bass
from concourse import mybir
from contextlib import ExitStack

P = 128
SEQS, STEPS, DIM = 8, 128, 256
TOK = SEQS * STEPS
CH = DIM // P
UNIT_SEQS = 2
UNITS = SEQS // UNIT_SEQS
UT = UNIT_SEQS * STEPS
PAD = STEPS + 1
SEGS = CH * UNIT_SEQS
EXPERTS, INNER, TOPK = 32, 96, 8
EG, IG = 4, 32
GROUPS = EXPERTS // EG
TILES = INNER // IG
HALVES = 2
HT = TOK // HALVES
STEPS_G = TILES * HALVES
TT = TOK // P
EPS = 1e-5
FAR = -1e38
K_, V_, R_, O_ = range(4)
BK, BV, BR, BO, TMK, TMV, TMR, U_, W_, XW, XU = range(11)


def build(nc, xT, ctxT, wproj, vecs, routerT, experts, eye, out):
    f32, f32r = mybir.dt.float32, mybir.dt.float32r
    ALU, ACT, AX = mybir.AluOpType, mybir.ActivationFunctionType, mybir.AxisListType
    ds = bass.ds
    es = ExitStack()
    with es:
        def sb(name, shape, dt=f32):
            return es.enter_context(nc.sbuf_tensor(name, shape, dt))

        def sem(name):
            return es.enter_context(nc.semaphore(name))

        x = sb("x", [P, CH, SEQS, PAD])
        ctx = sb("ctx", [P, CH, UNIT_SEQS, STEPS])
        dx = sb("dx", [P, CH, SEQS, STEPS])
        rmix = sb("rmix", [P, CH, SEQS, STEPS])
        x2 = sb("x2", [P, CH, TOK])
        x2h = sb("x2h", [P, CH, TOK], f32r)
        x2l = sb("x2l", [P, CH, TOK], f32r)
        wp = sb("wp", [P, 4, CH, DIM])
        vec = sb("vec", [P, 11, CH])
        rw = sb("rw", [P, CH, EXPERTS])
        ident = sb("ident", [P, P])
        avg = sb("avg", [P, P])
        eps = sb("eps", [P, 1])
        kw = sb("kw", [P, CH])
        wk = sb("wk", [P, CH])
        w2n = sb("w2n", [P, CH])
        xun = sb("xun", [P, CH])
        decay = sb("decay", [P, CH, UNIT_SEQS, PAD])

        work = sb("work", [P, 22, CH * UT])
        free = iter(range(22))

        def wb():
            return work[:, next(free), :].rearrange("p (c t) -> p c t", c=CH)

        kvmix = sb("kvmix", [P, 2, CH, UT])
        below = wb()
        above = wb()
        e2 = wb()
        e1 = wb()
        e2v = wb()
        num1 = wb()
        den1 = wb()
        rden1 = wb()
        wkv = wb()
        y1 = wb()
        x1 = sb("x1", [P, CH, UNIT_SEQS, PAD])

        o = sb("o", [P, SEGS, PAD])
        o_step = wb()
        k_o = wb()
        k_oprev = wb()
        a2 = sb("a2", [P, SEGS, PAD])
        ek = sb("ek", [P, SEGS, PAD])
        ekv = sb("ekv", [P, SEGS, PAD])
        pst = sb("pst", [P, SEGS, PAD])
        qst = sb("qst", [P, SEGS, PAD])
        lead = wb()
        lag = wb()
        aa = wb()
        ee = wb()
        ev = wb()
        ap_ = wb()
        aq = wb()
        num2 = wb()
        den2 = wb()
        lnd = sb("lnd", [P, CH, UT])
        rd0 = sb("rd0", [P, CH, UT])
        gd = sb("gd", [P, CH, UT])
        rdn = sb("rdn", [P, CH, UT])
        yn = sb("yn", [P, CH, UT])

        z = [sb(f"z{n}", [P, CH, UT]) for n in (1, 2)]
        cen = [sb(f"cen{n}", [P, CH, UT]) for n in (1, 2)]
        sq = [sb(f"sq{n}", [P, CH, UT]) for n in (1, 2)]
        lnv = [sb(f"lnv{n}", [P, UT]) for n in (1, 2)]
        r0 = [sb(f"r0{n}", [P, UT]) for n in (1, 2)]
        r0sq = [sb(f"r0sq{n}", [P, UT]) for n in (1, 2)]
        vr = [sb(f"vr{n}", [P, UT]) for n in (1, 2)]
        rn = [sb(f"rn{n}", [P, UT]) for n in (1, 2)]

        top = sb("top", [P, TT])
        shifted = sb("shifted", [P, TT, EXPERTS])
        ex = sb("ex", [P, TT, EXPERTS])
        zsum = sb("zsum", [P, TT])
        rz = sb("rz", [P, TT])
        probs = sb("probs", [P, TT, EXPERTS])
        best = sb("best", [P, TT, TOPK])
        marked = sb("marked", [P, TT, EXPERTS])
        chosen = sb("chosen", [P, TT, EXPERTS])
        csum = sb("csum", [P, TT])
        rcs = sb("rcs", [P, TT])
        gate = sb("gate", [P, TT, EXPERTS])
        gateT = sb("gateT", [EXPERTS, TOK])
        gates = work[:, 0:16, :].rearrange("p (g a) t -> p g (a t)", a=2)

        raw = [sb(f"raw{t}", [P, 3 * DIM]) for t in range(TILES)]
        whi = [sb(f"whi{t}", [P, 3 * DIM], f32r) for t in range(TILES)]
        wlo = [sb(f"wlo{t}", [P, 3 * DIM], f32r) for t in range(TILES)]
        sg = [work[:, 16 + i, :] for i in range(2)]
        sw = [work[:, 18 + i, :] for i in range(2)]
        h = [work[:, 20 + i, :] for i in range(2)]
        hh = [sb(f"hh{i}", [P, HT], f32r) for i in range(2)]
        hl = [sb(f"hl{i}", [P, HT], f32r) for i in range(2)]

        ps = es.enter_context(nc.psum_tensor("ps", [P, 8, 512], f32))
        k_ps, v_ps, r_ps, o_ps = (ps[:, i, :].rearrange("p (c t) -> p c t", c=CH) for i in range(4))
        ln_ps = [ps[:, 4, :], ps[:, 5, :]]

        flat = lambda t_: t_[:, :, :, :].rearrange("p c b s -> p c (b s)")
        z3, cen3, y3 = flat(dx), gates[:, 0:2, :], flat(rmix)
        sq3 = gates[:, 2:4, :]
        lnv3, r03, r0sq3, vr3 = (gates[:, 4 + i, :] for i in range(4))
        rn3 = lnv3

        s_x = [sem(f"x_in{i}") for i in range(2)]
        s_ctx = sem("ctx_in")
        s_small = sem("small_in")
        s_wp = sem("wp_in")
        names = """consts pads zeros dx rmixed silu_r kvmixed k_proj v_proj r_proj relu_k e2 e1 e2v
            num1 den1 rden1 wkv y1 o_proj x1 o_scan o_step k_o k_oprev a2 ek ekv relu_x aa ee ev
            p_scan q_scan ap aq num2 den2 lnd rd0 gd rdn yn x2 x2h x2l
            logits top shifted ex zsum rz probs best marked chosen csum rcs gate gateT_ps gateT
            w_hi w_lo g u silu sw h hh hl down out z3 mean3 cen3 sq3 var3 lnv3 r03 r0sq3 vr3 rn3
            y3""".split()
        s = {n: sem("s_" + n) for n in names}
        s_z, s_mean, s_cen, s_sq, s_var, s_lnv, s_r0, s_r0sq, s_vr, s_rn = (
            [sem(f"s_{n}{i}") for i in (1, 2)]
            for n in "z mean cen sq var lnv r0 r0sq vr rn".split())
        s_raw = [sem(f"raw{t}_in") for t in range(TILES)]
        s_gates = sem("gates_in")

        def need(eng, sm, n):
            if not isinstance(n, int) or n > 0:
                eng.wait_ge(sm, n)

        block = es.enter_context(nc.Block())

        @block.sync
        def _(sp):
            hs = SEQS // 2
            sp.wait_ge(s["pads"], 1)
            for c in range(CH):
                sp.dma_start(x[:, c, 0:hs, 1:PAD], xT[:, c, 0:hs, :]).then_inc(s_x[0], 16)
            sp.dma_start(vec[:, :, :], vecs).then_inc(s_small, 16)
            sp.dma_start(wp[:, :, :, :], wproj).then_inc(s_wp, 16)
            for c in range(CH):
                sp.dma_start(x[:, c, hs:SEQS, 1:PAD], xT[:, c, hs:SEQS, :]).then_inc(s_x[1], 16)
            sp.dma_start(rw[:, :, :], routerT).then_inc(s_small, 16)
            sp.dma_start(ident[:, :], eye).then_inc(s_small, 16)
            for t in range(TILES):
                sp.dma_start(raw[t][:, :], experts[0, t]).then_inc(s_raw[t], 16)
            sp.dma_start(ctx[:, :, :, :], ctxT[0]).then_inc(s_ctx, 16)
            with sp.Fori(1, UNITS) as u:
                sp.wait_ge(s["ev"], u)
                sp.dma_start(ctx[:, :, :, :], ctxT[ds(u, 1)].rearrange("a p c b s -> (a p) c b s")
                             ).then_inc(s_ctx, 16)

            def refill(m):
                for t in range(TILES):
                    sp.wait_ge(s["w_hi"], TILES * (m - 1) + t + 1)
                    sp.wait_ge(s["w_lo"], TILES * (m - 1) + t + 1)
                    src = experts[ds(m, 1), t].rearrange("a p n -> (a p) n")
                    sp.dma_start(raw[t][:, :], src).then_inc(s_raw[t], 16)

            with sp.Fori(1, GROUPS) as m:
                refill(m)
            for hf in range(HALVES):
                sp.wait_ge(s["y3"], hf + 1)
                sp.dma_start(out[:, :, hf * HT:(hf + 1) * HT],
                             rmix[:, :, :, :].rearrange("p c b s -> p c (b s)")[
                                 :, :, hf * HT:(hf + 1) * HT]).then_inc(s["out"], 16)
            sp.wait_ge(s["out"], 16 * HALVES)

        @block.gpsimd
        def _(pool):
            nc.gpsimd.memset(x[:, :, :, 0:1], 0.0).then_inc(s["pads"], 1)
            for t_ in (a2, ek, ekv):
                nc.gpsimd.memset(t_[:, :, 0:1], 0.0).then_inc(s["pads"], 1)

            def weigh1(u):
                pool.wait_ge(s["num1"], SEGS * (u + 1))
                pool.wait_ge(s["rden1"], u + 1)
                need(pool, s["y1"], CH * u)
                nc.gpsimd.tensor_tensor(wkv[:, :, :], num1[:, :, :], rden1[:, :, :],
                                        ALU.mult).then_inc(s["wkv"], 1)

            def shifts2(u):
                pool.wait_ge(s["o_scan"], u + 1)
                need(pool, s["ek"], u)
                need(pool, s["a2"], CH * u)
                need(pool, s["relu_x"], 2 * CH * u)
                op, on = o[:, :, 0:STEPS], o[:, :, 1:PAD]
                kx = x1[:, :, :, 1:PAD].rearrange("p c b s -> p (c b) s")
                seg = lambda t_: t_[:, :, :].rearrange("p c (b s) -> p (c b) s", s=STEPS)
                nc.gpsimd.tensor_tensor(seg(o_step), op, on, ALU.subtract).then_inc(s["o_step"], 1)
                nc.gpsimd.tensor_tensor(seg(k_o), kx, on, ALU.subtract).then_inc(s["k_o"], 1)
                nc.gpsimd.tensor_tensor(seg(k_oprev), kx, op, ALU.subtract).then_inc(s["k_oprev"], 1)

            def values2(u):
                cx = ctx[:, :, :, :].rearrange("p c b s -> p (c b) s")
                pool.wait_ge(s_ctx, 16 * (u + 1))
                pool.wait_ge(s["ek"], u + 1)
                need(pool, s["p_scan"], u)
                nc.gpsimd.tensor_tensor(ekv[:, :, 1:PAD], ek[:, :, 1:PAD], cx,
                                        ALU.mult).then_inc(s["ekv"], 1)
                pool.wait_ge(s["ekv"], u + 1)
                pool.wait_ge(s["ee"], u + 1)
                need(pool, s["num2"], u)
                seg = lambda t_: t_[:, :, :].rearrange("p c (b s) -> p (c b) s", s=STEPS)
                nc.gpsimd.tensor_tensor(seg(ev), seg(ee), cx, ALU.mult).then_inc(s["ev"], 1)

            weigh1(0)

            def both(i):
                shifts2(i)
                values2(i)
                weigh1(i + 1)

            both(0)
            with pool.Fori(1, UNITS - 1) as i:
                both(i)
            shifts2(UNITS - 1)
            values2(UNITS - 1)

            def rest_w(m, t):
                pool.wait_ge(s["w_hi"], TILES * m + t + 1)
                nc.gpsimd.tensor_tensor(wlo[t][:, :], raw[t][:, :], whi[t][:, :].bitcast(f32),
                                        ALU.subtract).then_inc(s["w_lo"], 1)

            for t in range(TILES):
                rest_w(0, t)
            with pool.Fori(1, GROUPS) as m:
                for t in range(TILES):
                    rest_w(m, t)

        @block.scalar
        def _(act):
            act.wait_ge(s["rmixed"], CH)
            hs = SEQS // 2
            for hf in range(2):
                act.wait_ge(s["rmixed"], CH * (hf + 1))
                v_ = rmix[:, :, hf * hs:(hf + 1) * hs, :]
                nc.scalar.activation(v_, v_, ACT.Silu).then_inc(s["silu_r"], 1)
            act.preload_act_table_set("natural_log_exp_and_others")
            act.wait_ge(s["consts"], 5)

            def exps1(u):
                act.wait_ge(s["k_proj"], u + 1)
                for c in range(CH):
                    nc.scalar.activation(below[:, c, :], k_ps[:, c, :], ACT.Relu, bias=wk[:, c:c + 1],
                                         scale=-1.0).then_inc(s["relu_k"], 1)
                for c in range(CH):
                    nc.scalar.activation(above[:, c, :], k_ps[:, c, :], ACT.Relu, bias=kw[:, c:c + 1],
                                         scale=1.0).then_inc(s["relu_k"], 1)
                act.wait_ge(s["relu_k"], 2 * CH * u + CH)
                need(act, s["den1"], SEGS * u)
                nc.scalar.activation(e2[:, :, :], below[:, :, :], ACT.Exp, scale=-1.0).then_inc(s["e2"], 1)
                act.wait_ge(s["relu_k"], 2 * CH * (u + 1))
                for c in range(CH):
                    nc.scalar.activation(e1[:, c, :], above[:, c, :], ACT.Exp, bias=w2n[:, c:c + 1],
                                         scale=-1.0).then_inc(s["e1"], 1)

            def exps2(u):
                seg2 = lambda t_, c: t_[:, UNIT_SEQS * c:UNIT_SEQS * (c + 1), 1:PAD]
                b2 = lambda t_, c: t_[:, c, :].rearrange("p (b s) -> p b s", s=STEPS)
                act.wait_ge(s["o_step"], u + 1)
                need(act, s["q_scan"], u)
                for c in range(CH):
                    nc.scalar.activation(seg2(a2, c), b2(o_step, c), ACT.Exp,
                                         bias=vec[:, XW, c:c + 1]).then_inc(s["a2"], 1)
                act.wait_ge(s["k_o"], u + 1)
                nc.scalar.activation(ek[:, :, 1:PAD],
                                     k_o[:, :, :].rearrange("p c (b s) -> p (c b) s", s=STEPS),
                                     ACT.Exp).then_inc(s["ek"], 1)
                act.wait_ge(s["k_oprev"], u + 1)
                for c in range(CH):
                    nc.scalar.activation(lead[:, c, :], k_oprev[:, c, :], ACT.Relu,
                                         bias=vec[:, XU, c:c + 1]).then_inc(s["relu_x"], 1)
                    nc.scalar.activation(lag[:, c, :], k_oprev[:, c, :], ACT.Relu, scale=-1.0,
                                         bias=xun[:, c:c + 1]).then_inc(s["relu_x"], 1)
                act.wait_ge(s["relu_x"], 2 * CH * (u + 1))
                need(act, s["den2"], u)
                need(act, s["ev"], u)
                nc.scalar.activation(ee[:, :, :], lag[:, :, :], ACT.Exp, scale=-1.0).then_inc(s["ee"], 1)
                nc.scalar.activation(aa[:, :, :], lead[:, :, :], ACT.Exp, scale=-1.0).then_inc(s["aa"], 1)

            def first_rden2(u):
                act.wait_ge(s["den2"], u + 1)
                nc.scalar.activation(lnd[:, :, :], den2[:, :, :], ACT.Ln).then_inc(s["lnd"], 1)
                act.wait_ge(s["lnd"], u + 1)
                nc.scalar.activation(rd0[:, :, :], lnd[:, :, :], ACT.Exp, scale=-1.0).then_inc(s["rd0"], 1)

            def square(n, u):
                act.wait_ge(s_cen[n], u + 1)
                need(act, s_var[n], u)
                nc.scalar.activation(sq[n][:, :, :], cen[n][:, :, :], ACT.Square).then_inc(s_sq[n], 1)

            def first_rstd(n, u):
                act.wait_ge(s_var[n], u + 1)
                nc.scalar.activation(lnv[n][:, :], ln_ps[n][:, UT:2 * UT], ACT.Ln,
                                     bias=eps[:, :]).then_inc(s_lnv[n], 1)
                act.wait_ge(s_lnv[n], u + 1)
                nc.scalar.activation(r0[n][:, :], lnv[n][:, :], ACT.Exp, scale=-0.5).then_inc(s_r0[n], 1)
                act.wait_ge(s_r0[n], u + 1)
                nc.scalar.activation(r0sq[n][:, :], r0[n][:, :], ACT.Square).then_inc(s_r0sq[n], 1)

            def upper_x2(u):
                act.wait_ge(s["x2"], u + 1)
                at = ds(u * UT, UT)
                nc.scalar.activation(x2h[:, :, at], x2[:, :, at], ACT.Copy).then_inc(s["x2h"], 1)

            exps1(0)
            square(0, 0)
            first_rstd(0, 0)

            def both(i):
                exps1(i + 1)
                exps2(i)
                first_rden2(i)
                square(1, i)
                square(0, i + 1)
                first_rstd(1, i)
                first_rstd(0, i + 1)
                upper_x2(i)

            both(0)
            with act.Fori(1, UNITS - 1) as i:
                both(i)
            exps2(UNITS - 1)
            first_rden2(UNITS - 1)
            square(1, UNITS - 1)
            first_rstd(1, UNITS - 1)
            upper_x2(UNITS - 1)

            def upper_w(m, t):
                act.wait_ge(s_raw[t], 16 * (m + 1))
                need(act, s["down"], STEPS_G * (m - 1) + HALVES * (t + 1))
                nc.scalar.activation(whi[t][:, :], raw[t][:, :], ACT.Copy).then_inc(s["w_hi"], 1)

            for t in range(TILES):
                upper_w(0, t)
            act.wait_ge(s["shifted"], 1)
            nc.scalar.activation(ex[:, :, :], shifted[:, :, :], ACT.Exp).then_inc(s["ex"], 1)

            def expert_steps(m, last):
                for st in range(STEPS_G):
                    n = STEPS_G * m + st
                    i = st % 2
                    act.wait_ge(s["g"], n + 1)
                    need(act, s["sw"], n - 1)
                    nc.scalar.activation(sg[i][:, :], ps[:, 4 + 2 * i, :], ACT.Silu).then_inc(s["silu"], 1)
                    if isinstance(m, int) and m == 0 and st == 0:
                        for hf in range(HALVES):
                            act.wait_ge(s["gateT_ps"], 1)
                            nc.scalar.activation(gateT[:, hf * HT:(hf + 1) * HT], ps[0:EXPERTS, 2 * hf, :],
                                                 ACT.Copy).then_inc(s["gateT"], 1)
                        act.wait_ge(s["gateT"], HALVES)
                        for gr in range(GROUPS):
                            act.dma_start(gates[:, gr, :],
                                          gateT[EG * gr:EG * (gr + 1), :].unsqueeze(1).to_broadcast(
                                              [EG, IG, TOK])).then_inc(s_gates, 16)
                    act.wait_ge(s["h"], n + 1)
                    need(act, s["down"], n - 1)
                    nc.scalar.activation(hh[i][:, :], h[i][:, :], ACT.Copy).then_inc(s["hh"], 1)
                    if st == 0:
                        if not (isinstance(m, int) and m == 0):
                            upper_w(m, TILES - 1)
                    elif st % 2 == 0 and not last:
                        upper_w(m + 1, st // 2 - 1)

            expert_steps(0, False)
            with act.Fori(1, GROUPS - 1) as m:
                expert_steps(m, False)
            expert_steps(GROUPS - 1, True)

            act.preload_act_table_set("natural_log_exp_and_others")
            for hf in range(HALVES):
                at = slice(hf * HT, (hf + 1) * HT)
                act.wait_ge(s["cen3"], hf + 1)
                nc.scalar.activation(sq3[:, :, at], cen3[:, :, at], ACT.Square).then_inc(s["sq3"], 1)
                act.wait_ge(s["var3"], hf + 1)
                nc.scalar.activation(lnv3[:, at], ps[:, 6 + hf, :], ACT.Ln, bias=eps[:, :]).then_inc(s["lnv3"], 1)
                act.wait_ge(s["lnv3"], hf + 1)
                nc.scalar.activation(r03[:, at], lnv3[:, at], ACT.Exp, scale=-0.5).then_inc(s["r03"], 1)
                act.wait_ge(s["r03"], hf + 1)
                nc.scalar.activation(r0sq3[:, at], r03[:, at], ACT.Square).then_inc(s["r0sq3"], 1)

        @block.vector
        def _(dve):
            nc.vector.memset(avg[:, :], 1.0 / DIM).then_inc(s["consts"], 1)
            nc.vector.memset(eps[:, :], EPS).then_inc(s["zeros"], 1)
            nc.vector.memset(x1[:, :, :, 0:1], FAR).then_inc(s["zeros"], 1)
            nc.vector.memset(decay[:, :, :, :], 0.0).then_inc(s["zeros"], 1)
            dve.wait_ge(s_small, 16 * 3)
            v = lambda i: vec[:, i, :]
            nc.vector.tensor_tensor(kw[:, :], v(BK), v(U_), ALU.add).then_inc(s["zeros"], 1)
            dve.wait_ge(s["zeros"], 4)
            nc.vector.tensor_tensor(wk[:, :], v(W_), kw[:, :], ALU.subtract).then_inc(s["consts"], 1)
            dve.wait_ge(s["consts"], 2)
            nc.vector.tensor_scalar(kw[:, :], wk[:, :], -1.0, None, ALU.mult).then_inc(s["consts"], 1)
            nc.vector.tensor_scalar(w2n[:, :], v(W_), -2.0, None, ALU.mult).then_inc(s["consts"], 1)
            nc.vector.tensor_scalar(xun[:, :], v(XU), -1.0, None, ALU.mult).then_inc(s["consts"], 1)
            for c in range(CH):
                nc.vector.tensor_scalar(decay[:, c, :, :], decay[:, c, :, :], vec[:, XW, c:c + 1], None,
                                        ALU.add).then_inc(s["zeros"], 1)
            dve.wait_ge(s["zeros"], 4 + CH)
            nc.vector.memset(decay[:, :, :, 0:1], FAR).then_inc(s["zeros"], 1)

            hs = SEQS // 2

            def mix_r(hf):
                sl = slice(hf * hs, (hf + 1) * hs)
                dve.wait_ge(s_x[hf], 16 * CH)
                nc.vector.tensor_tensor(dx[:, :, sl, :], x[:, :, sl, 1:PAD], x[:, :, sl, 0:STEPS],
                                        ALU.subtract).then_inc(s["dx"], 1)
                dve.wait_ge(s["dx"], hf + 1)
                for c in range(CH):
                    nc.vector.scalar_tensor_tensor(rmix[:, c, sl, :], dx[:, c, sl, :], vec[:, TMR, c:c + 1],
                                                   x[:, c, sl, 0:STEPS], ALU.mult,
                                                   ALU.add).then_inc(s["rmixed"], 1)

            def mix_kv(u):
                need(dve, s["v_proj"], u)
                seqs = ds(u * UNIT_SEQS, UNIT_SEQS)
                for n, tm in enumerate((TMK, TMV)):
                    for c in range(CH):
                        nc.vector.scalar_tensor_tensor(
                            kvmix[:, n, c, :].rearrange("p (b s) -> p b s", s=STEPS), dx[:, c, seqs, :],
                            vec[:, tm, c:c + 1], x[:, c, seqs, 0:STEPS], ALU.mult,
                            ALU.add).then_inc(s["kvmixed"], 1)

            def scans1(u):
                dve.wait_ge(s["v_proj"], u + 1)
                dve.wait_ge(s["e2"], u + 1)
                for c in range(CH):
                    nc.vector.scalar_tensor_tensor(e2v[:, c, :], v_ps[:, c, :], vec[:, BV, c:c + 1],
                                                   e2[:, c, :], ALU.add, ALU.mult).then_inc(s["e2v"], 1)
                dve.wait_ge(s["e1"], CH * (u + 1))
                need(dve, s["wkv"], u)
                segs = [(c, slice(b * STEPS, (b + 1) * STEPS)) for c in range(CH) for b in range(UNIT_SEQS)]
                for c, at in segs:
                    nc.vector.tensor_tensor_scan(den1[:, c, at], e1[:, c, at], e2[:, c, at], 0.0,
                                                 ALU.mult, ALU.add).then_inc(s["den1"], 1)
                dve.wait_ge(s["e2v"], CH * (u + 1))
                for c, at in segs:
                    nc.vector.tensor_tensor_scan(num1[:, c, at], e1[:, c, at], e2v[:, c, at], 0.0,
                                                 ALU.mult, ALU.add).then_inc(s["num1"], 1)
                dve.wait_ge(s["den1"], SEGS * (u + 1))
                nc.vector.reciprocal(rden1[:, :, :], den1[:, :, :]).then_inc(s["rden1"], 1)

            def times_r(u):
                dve.wait_ge(s["r_proj"], u + 1)
                dve.wait_ge(s["wkv"], u + 1)
                need(dve, s["o_proj"], u)
                for c in range(CH):
                    nc.vector.scalar_tensor_tensor(y1[:, c, :], r_ps[:, c, :], vec[:, BR, c:c + 1],
                                                   wkv[:, c, :], ALU.add, ALU.mult).then_inc(s["y1"], 1)

            def residual1(u):
                dve.wait_ge(s["o_proj"], u + 1)
                need(dve, s_mean[0], u)
                seqs = ds(u * UNIT_SEQS, UNIT_SEQS)
                bs = lambda t_: t_.rearrange("p (b s) -> p b s", s=STEPS)
                for c in range(CH):
                    nc.vector.scalar_tensor_tensor(bs(z[0][:, c, :]), bs(o_ps[:, c, :]),
                                                   vec[:, BO, c:c + 1], x[:, c, seqs, 1:PAD], ALU.add,
                                                   ALU.add).then_inc(s_z[0], 1)

            def center(n, u):
                dve.wait_ge(s_mean[n], u + 1)
                mean = ln_ps[n][:, 0:UT].unsqueeze(1).to_broadcast([P, CH, UT])
                nc.vector.tensor_tensor(cen[n][:, :, :], z[n][:, :, :], mean,
                                        ALU.subtract).then_inc(s_cen[n], 1)

            def newton_rstd(n, u):
                dve.wait_ge(s_r0sq[n], u + 1)
                nc.vector.scalar_tensor_tensor(vr[n][:, :], ln_ps[n][:, UT:2 * UT], EPS, r0sq[n][:, :],
                                               ALU.add, ALU.mult).then_inc(s_vr[n], 1)
                dve.wait_ge(s_vr[n], u + 1)
                nc.vector.scalar_tensor_tensor(rn[n][:, :], vr[n][:, :], -3.0, r0[n][:, :],
                                               ALU.add, ALU.mult).then_inc(s_rn[n], 1)
                dve.wait_ge(s_rn[n], u + 1)

            def norm1(u):
                newton_rstd(0, u)
                bs = lambda t_: t_.rearrange("p (b s) -> p b s", s=STEPS)
                for c in range(CH):
                    nc.vector.scalar_tensor_tensor(x1[:, c, :, 1:PAD], bs(cen[0][:, c, :]), -0.5,
                                                   bs(rn[0][:, :]), ALU.mult, ALU.mult).then_inc(s["x1"], 1)

            def norm2(u):
                newton_rstd(1, u)
                nc.vector.scalar_tensor_tensor(x2[:, :, ds(u * UT, UT)], cen[1][:, :, :], -0.5,
                                               rn[1][:, :].unsqueeze(1).to_broadcast([P, CH, UT]),
                                               ALU.mult, ALU.mult).then_inc(s["x2"], 1)

            def rest_x2(u):
                dve.wait_ge(s["x2h"], u + 1)
                cols = ds(u * UT, UT)
                nc.vector.tensor_tensor(x2l[:, :, cols], x2[:, :, cols], x2h[:, :, cols].bitcast(f32),
                                        ALU.subtract).then_inc(s["x2l"], 1)

            def max_scan(u):
                dve.wait_ge(s["x1"], CH * (u + 1))
                nc.vector.tensor_tensor_scan(
                    o[:, :, :].rearrange("p g s -> p (g s)"),
                    decay[:, :, :, :].rearrange("p c b s -> p (c b s)"),
                    x1[:, :, :, :].rearrange("p c b s -> p (c b s)"), FAR, ALU.add,
                    ALU.max).then_inc(s["o_scan"], 1)

            def scans2(u):
                line = lambda t_: t_[:, :, :].rearrange("p g s -> p (g s)")
                dve.wait_ge(s["a2"], CH * (u + 1))
                dve.wait_ge(s["ek"], u + 1)
                nc.vector.tensor_tensor_scan(line(qst), line(a2), line(ek), 0.0, ALU.mult,
                                             ALU.add).then_inc(s["q_scan"], 1)
                dve.wait_ge(s["ekv"], u + 1)
                nc.vector.tensor_tensor_scan(line(pst), line(a2), line(ekv), 0.0, ALU.mult,
                                             ALU.add).then_inc(s["p_scan"], 1)

            def outputs2(u):
                seg = lambda t_: t_[:, :, :].rearrange("p c (b s) -> p (c b) s", s=STEPS)
                dve.wait_ge(s["aa"], u + 1)
                dve.wait_ge(s["q_scan"], u + 1)
                nc.vector.tensor_tensor(seg(aq), seg(aa), qst[:, :, 0:STEPS], ALU.mult).then_inc(s["aq"], 1)
                dve.wait_ge(s["p_scan"], u + 1)
                nc.vector.tensor_tensor(seg(ap_), seg(aa), pst[:, :, 0:STEPS], ALU.mult).then_inc(s["ap"], 1)
                dve.wait_ge(s["aq"], u + 1)
                nc.vector.tensor_tensor(den2[:, :, :], aq[:, :, :], ee[:, :, :], ALU.add).then_inc(s["den2"], 1)
                dve.wait_ge(s["ap"], u + 1)
                dve.wait_ge(s["ev"], u + 1)
                nc.vector.tensor_tensor(num2[:, :, :], ap_[:, :, :], ev[:, :, :], ALU.add).then_inc(s["num2"], 1)

            def residual2(u):
                dve.wait_ge(s["rd0"], u + 1)
                nc.vector.tensor_tensor(gd[:, :, :], den2[:, :, :], rd0[:, :, :], ALU.mult).then_inc(s["gd"], 1)
                dve.wait_ge(s["gd"], u + 1)
                nc.vector.scalar_tensor_tensor(rdn[:, :, :], gd[:, :, :], -2.0, rd0[:, :, :], ALU.add,
                                               ALU.mult).then_inc(s["rdn"], 1)
                dve.wait_ge(s["rdn"], u + 1)
                dve.wait_ge(s["num2"], u + 1)
                nc.vector.tensor_tensor(yn[:, :, :], num2[:, :, :], rdn[:, :, :], ALU.mult).then_inc(s["yn"], 1)
                dve.wait_ge(s["yn"], u + 1)
                need(dve, s_mean[1], u)
                seg = lambda t_: t_[:, :, :].rearrange("p c (b s) -> p (c b) s", s=STEPS)
                nc.vector.scalar_tensor_tensor(seg(z[1]), seg(yn), -1.0,
                                               x1[:, :, :, 1:PAD].rearrange("p c b s -> p (c b) s"),
                                               ALU.mult, ALU.add).then_inc(s_z[1], 1)

            mix_r(0)
            mix_kv(0)
            mix_r(1)
            scans1(0)
            times_r(0)
            residual1(0)
            center(0, 0)
            norm1(0)

            def both(i):
                mix_kv(i + 1)
                max_scan(i)
                scans1(i + 1)
                scans2(i)
                outputs2(i)
                times_r(i + 1)
                residual2(i)
                residual1(i + 1)
                center(1, i)
                center(0, i + 1)
                norm2(i)
                norm1(i + 1)
                rest_x2(i)

            dve.wait_ge(s["zeros"], 5 + CH)
            dve.wait_ge(s["pads"], 4)
            both(0)
            with dve.Fori(1, UNITS - 1) as i:
                both(i)
            last = UNITS - 1
            max_scan(last)
            scans2(last)
            outputs2(last)
            residual2(last)
            center(1, last)
            norm2(last)
            rest_x2(last)

            wide = lambda t_: t_[:, :].unsqueeze(2).to_broadcast([P, TT, EXPERTS])
            logits = ps[:, 0, 0:TT * EXPERTS].rearrange("p (t e) -> p t e", t=TT)
            dve.wait_ge(s["logits"], 1)
            nc.vector.tensor_reduce(top[:, :], logits, AX.X, ALU.max).then_inc(s["top"], 1)
            dve.wait_ge(s["top"], 1)
            nc.vector.tensor_tensor(shifted[:, :, :], logits, wide(top), ALU.subtract).then_inc(s["shifted"], 1)
            dve.wait_ge(s["ex"], 1)
            nc.vector.tensor_reduce(zsum[:, :], ex[:, :, :], AX.X, ALU.add).then_inc(s["zsum"], 1)
            dve.wait_ge(s["zsum"], 1)
            nc.vector.reciprocal(rz[:, :], zsum[:, :]).then_inc(s["rz"], 1)
            dve.wait_ge(s["rz"], 1)
            nc.vector.tensor_tensor(probs[:, :, :], ex[:, :, :], wide(rz), ALU.mult).then_inc(s["probs"], 1)
            dve.wait_ge(s["probs"], 1)
            for t in range(TT):
                nc.vector.max(best[:, t, :], probs[:, t, :]).then_inc(s["best"], 1)
            for t in range(TT):
                dve.wait_ge(s["best"], t + 1)
                nc.vector.match_replace(marked[:, t, :], best[:, t, :], probs[:, t, :],
                                        -1.0).then_inc(s["marked"], 1)
            dve.wait_ge(s["marked"], TT)
            nc.vector.scalar_tensor_tensor(chosen[:, :, :], marked[:, :, :], 0.0, probs[:, :, :],
                                           ALU.is_lt, ALU.mult).then_inc(s["chosen"], 1)
            dve.wait_ge(s["chosen"], 1)
            nc.vector.tensor_reduce(csum[:, :], chosen[:, :, :], AX.X, ALU.add).then_inc(s["csum"], 1)
            dve.wait_ge(s["csum"], 1)
            nc.vector.reciprocal(rcs[:, :], csum[:, :]).then_inc(s["rcs"], 1)
            dve.wait_ge(s["rcs"], 1)
            nc.vector.tensor_tensor(gate[:, :, :], chosen[:, :, :], wide(rcs), ALU.mult).then_inc(s["gate"], 1)

            def expert_steps(m):
                for st in range(STEPS_G):
                    n = STEPS_G * m + st
                    i, hf = st % 2, st % HALVES
                    dve.wait_ge(s["silu"], n + 1)
                    nc.vector.tensor_tensor(sw[i][:, :], sg[i][:, :],
                                            gates[:, ds(m, 1), hf * HT:(hf + 1) * HT],
                                            ALU.mult).then_inc(s["sw"], 1)
                    dve.wait_ge(s["sw"], n + 1)
                    dve.wait_ge(s["u"], n + 1)
                    nc.vector.tensor_tensor(h[i][:, :], ps[:, 5 + 2 * i, :], sw[i][:, :],
                                            ALU.mult).then_inc(s["h"], 1)
                    dve.wait_ge(s["hh"], n + 1)
                    need(dve, s["down"], n - 1)
                    nc.vector.tensor_tensor(hl[i][:, :], h[i][:, :], hh[i][:, :].bitcast(f32),
                                            ALU.subtract).then_inc(s["hl"], 1)

            dve.wait_ge(s_gates, 16 * GROUPS)
            expert_steps(0)
            with dve.Fori(1, GROUPS) as m:
                expert_steps(m)

            cols = [slice(hf * HT, (hf + 1) * HT) for hf in range(HALVES)]
            for hf, at in enumerate(cols):
                dve.wait_ge(s["down"], STEPS_G * GROUPS - 1 + hf)
                nc.vector.tensor_tensor(z3[:, :, at], ps[:, 2 * hf:2 * hf + 2, :], x2[:, :, at],
                                        ALU.add).then_inc(s["z3"], 1)
            for hf, at in enumerate(cols):
                dve.wait_ge(s["mean3"], hf + 1)
                nc.vector.tensor_tensor(cen3[:, :, at], z3[:, :, at],
                                        ps[:, 4 + hf, :].unsqueeze(1).to_broadcast([P, CH, HT]),
                                        ALU.subtract).then_inc(s["cen3"], 1)
            for hf, at in enumerate(cols):
                dve.wait_ge(s["r0sq3"], hf + 1)
                nc.vector.scalar_tensor_tensor(vr3[:, at], ps[:, 6 + hf, :], EPS, r0sq3[:, at], ALU.add,
                                               ALU.mult).then_inc(s["vr3"], 1)
                dve.wait_ge(s["vr3"], hf + 1)
                nc.vector.scalar_tensor_tensor(rn3[:, at], vr3[:, at], -3.0, r03[:, at], ALU.add,
                                               ALU.mult).then_inc(s["rn3"], 1)
                dve.wait_ge(s["rn3"], hf + 1)
                nc.vector.scalar_tensor_tensor(y3[:, :, at], cen3[:, :, at], -0.5,
                                               rn3[:, at].unsqueeze(1).to_broadcast([P, CH, HT]),
                                               ALU.mult, ALU.mult).then_inc(s["y3"], 1)

        @block.tensor
        def _(pe):
            mm = nc.tensor.matmul

            def project(dst, which, src):
                for mo in range(CH):
                    for k in range(CH):
                        last = mm(dst[:, mo, :], wp[:, which, k, mo * P:(mo + 1) * P], src(k),
                                  start=(k == 0), stop=(k == CH - 1))
                return last

            def projections(u):
                pe.wait_ge(s["kvmixed"], 2 * CH * u + CH)
                need(pe, s["relu_k"], 2 * CH * u)
                project(k_ps, K_, lambda k: kvmix[:, 0, k, :]).then_inc(s["k_proj"], 1)
                pe.wait_ge(s["kvmixed"], 2 * CH * (u + 1))
                need(pe, s["e2v"], CH * u)
                project(v_ps, V_, lambda k: kvmix[:, 1, k, :]).then_inc(s["v_proj"], 1)
                need(pe, s["y1"], CH * u)
                seqs = ds(u * UNIT_SEQS, UNIT_SEQS)
                project(r_ps, R_, lambda k: rmix[:, k, seqs, :]).then_inc(s["r_proj"], 1)

            def project_out(u):
                pe.wait_ge(s["y1"], CH * (u + 1))
                need(pe, s_z[0], CH * u)
                project(o_ps, O_, lambda k: y1[:, k, :]).then_inc(s["o_proj"], 1)

            def mean(n, u, per):
                pe.wait_ge(s_z[n], per * (u + 1))
                need(pe, s_vr[n], u)
                for k in range(CH):
                    last = mm(ln_ps[n][:, 0:UT], avg[:, :], z[n][:, k, :], start=(k == 0), stop=(k == CH - 1))
                last.then_inc(s_mean[n], 1)

            def variance(n, u):
                pe.wait_ge(s_sq[n], u + 1)
                for k in range(CH):
                    last = mm(ln_ps[n][:, UT:2 * UT], avg[:, :], sq[n][:, k, :], start=(k == 0), stop=(k == CH - 1))
                last.then_inc(s_var[n], 1)

            pe.wait_ge(s_wp, 16)
            pe.wait_ge(s["consts"], 1)
            pe.wait_ge(s["silu_r"], 2)
            projections(0)
            project_out(0)
            mean(0, 0, CH)
            variance(0, 0)

            def both(i):
                projections(i + 1)
                project_out(i + 1)
                mean(1, i, 1)
                mean(0, i + 1, CH)
                variance(1, i)
                variance(0, i + 1)

            both(0)
            with pe.Fori(1, UNITS - 1) as i:
                both(i)
            mean(1, UNITS - 1, 1)
            variance(1, UNITS - 1)

            pe.wait_ge(s["x2"], UNITS)
            for t in range(TT):
                for k in range(CH):
                    last = mm(ps[:, 0, t * EXPERTS:(t + 1) * EXPERTS], x2[:, k, t * P:(t + 1) * P],
                              rw[:, k, :], start=(k == 0), stop=(k == CH - 1))
            last.then_inc(s["logits"], 1)
            pe.wait_ge(s["x2h"], UNITS)
            pe.wait_ge(s["x2l"], UNITS)
            pe.wait_ge(s_vr[0], UNITS)
            pe.wait_ge(s_vr[1], UNITS)

            def up(m, st):
                t, hf, i = st // HALVES, st % HALVES, st % 2
                n = STEPS_G * m + st
                if hf == 0:
                    pe.wait_ge(s["w_hi"], TILES * m + t + 1)
                    pe.wait_ge(s["w_lo"], TILES * m + t + 1)
                for which, bank, done in ((0, 4 + 2 * i, "g"), (1, 5 + 2 * i, "u")):
                    need(pe, s["silu" if which == 0 else "h"], n - 1)
                    parts = [(k, w_, x_) for k in range(CH) for w_, x_ in
                             ((whi, x2h), (whi, x2l), (wlo, x2h))]
                    for j, (k, w_, x_) in enumerate(parts):
                        a = which * DIM + k * P
                        last = mm(ps[:, bank, :], w_[t][:, a:a + P], x_[:, k, hf * HT:(hf + 1) * HT],
                                  start=(j == 0), stop=(j == len(parts) - 1))
                    last.then_inc(s[done], 1)

            def down(m, st, first, final):
                t, hf, i = st // HALVES, st % HALVES, st % 2
                n = STEPS_G * m + st
                pe.wait_ge(s["hh"], n + 1)
                pe.wait_ge(s["hl"], n + 1)
                for mo in range(CH):
                    a = 2 * DIM + mo * P
                    for j, (w_, h_) in enumerate(((whi, hh), (whi, hl), (wlo, hh))):
                        last = mm(ps[:, 2 * hf + mo, :], w_[t][:, a:a + P], h_[i][:, :],
                                  start=(first and j == 0), stop=(final and j == 2))
                last.then_inc(s["down"], 1)

            def expert_steps(m, first, final):
                for st in range(STEPS_G):
                    up(m, st)
                    if st == 0:
                        if not first:
                            down(m - 1, STEPS_G - 1, False, False)
                    else:
                        if first and st == 1:
                            pass
                        down(m, st - 1, first and st - 1 < HALVES, False if not final else st - 1 >= STEPS_G - HALVES)

            up(0, 0)
            pe.wait_ge(s["gate"], 1)
            for t in range(TT):
                bank, a = 2 * (t // (TT // HALVES)), (t % (TT // HALVES)) * P
                last = nc.tensor.transpose(ps[0:EXPERTS, bank, a:a + P], gate[:, t, :], ident[:, :])
            last.then_inc(s["gateT_ps"], 1)
            pe.wait_ge(s["gateT"], HALVES)
            for st in range(1, STEPS_G):
                up(0, st)
                down(0, st - 1, st - 1 < HALVES, False)
            with pe.Fori(1, GROUPS - 1) as m:
                expert_steps(m, False, False)
            expert_steps(GROUPS - 1, False, True)
            down(GROUPS - 1, STEPS_G - 1, False, True)

            for hf in range(HALVES):
                pe.wait_ge(s["z3"], hf + 1)
                for k in range(CH):
                    last = mm(ps[:, 4 + hf, :], avg[:, :], z3[:, k, hf * HT:(hf + 1) * HT],
                              start=(k == 0), stop=(k == CH - 1))
                last.then_inc(s["mean3"], 1)
            for hf in range(HALVES):
                pe.wait_ge(s["sq3"], hf + 1)
                for k in range(CH):
                    last = mm(ps[:, 6 + hf, :], avg[:, :], sq3[:, k, hf * HT:(hf + 1) * HT],
                              start=(k == 0), stop=(k == CH - 1))
                last.then_inc(s["var3"], 1)


def kernel(**inputs):
    import numpy as np
    import concourse.bacc as bacc
    from concourse.bass_utils import run_bass_kernel_spmd as run

    a = {n: np.asarray(v) for n, v in inputs.items()}
    at = {n[len("L0_attn_"):]: v for n, v in a.items() if n.startswith("L0_attn_")}

    def channels(t):
        return t.reshape(SEQS, STEPS, CH, P).transpose(3, 2, 0, 1)

    def rows(w):
        return w.T.reshape(CH, P, -1).transpose(1, 0, 2)

    vectors = [at["bk"], at["bv"], at["br"], at["bo"], at["tmk"], at["tmv"], at["tmr"], at["u"],
               at["w"], a["L0_xattn_w"], a["L0_xattn_u"]]

    def up_rows(w):
        w = w.reshape(GROUPS, EG, CH, P, TILES, IG).transpose(0, 4, 3, 2, 1, 5)
        return w.reshape(GROUPS, TILES, P, CH * P)

    down_rows = a["L0_ffn_w_down"].reshape(GROUPS, EG, TILES, IG, DIM).transpose(0, 2, 1, 3, 4)
    arrays = {
        "xT": channels(a["x"]),
        "ctxT": channels(a["ctx_2048"]).reshape(P, CH, UNITS, UNIT_SEQS, STEPS).transpose(2, 0, 1, 3, 4),
        "wproj": np.stack([rows(at[n]) for n in ("Wk", "Wv", "Wr", "Wo")], axis=1),
        "vecs": np.stack([v.reshape(CH, P).T for v in vectors], axis=1),
        "routerT": rows(a["L0_ffn_router_w"]),
        "experts": np.concatenate([up_rows(a["L0_ffn_w_gate"]), up_rows(a["L0_ffn_w_up"]),
                                   down_rows.reshape(GROUPS, TILES, P, DIM)], axis=3),
        "eye": np.eye(P, dtype=np.float32),
    }
    arrays = {n: np.ascontiguousarray(v) for n, v in arrays.items()}
    nc = bacc.Bacc("TRN2", target_bir_lowering=False, num_devices=1)
    args = [nc.dram_tensor(f"in_{n}", v.shape, mybir.dt.from_np(v.dtype), kind="ExternalInput").ap()
            for n, v in arrays.items()]
    out = nc.dram_tensor("out", (P, CH, TOK), mybir.dt.float32, kind="ExternalOutput").ap()
    build(nc, *args, out)
    r = run(nc, [{f"in_{n}": v for n, v in arrays.items()}], core_ids=[0])
    y = np.asarray(r.results[0]["out"])
    return y.transpose(2, 1, 0).reshape(SEQS, STEPS, DIM)
```

```python
import concourse.bass as bass
from concourse import mybir
from contextlib import ExitStack

P = 128
SEQS, STEPS, DIM = 8, 128, 256
TOK = SEQS * STEPS
CH = DIM // P
UNIT_SEQS = 2
UNITS = SEQS // UNIT_SEQS
UT = UNIT_SEQS * STEPS
PAD = STEPS + 1
SEGS = CH * UNIT_SEQS
EXPERTS, INNER, TOPK = 32, 96, 8
EG, IG = 4, 32
GROUPS = EXPERTS // EG
TILES = INNER // IG * GROUPS
SLOTS = 4
HALVES = 2
HT = TOK // HALVES
STEPS_ALL = HALVES * TILES
TH = HT // P
EPS = 1e-5
FAR = -1e38
K_, V_, R_, O_ = range(4)
BK, BV, BR, BO, TMK, TMV, TMR, U_, W_, XW, XU = range(11)


def build(nc, xT, ctxT, wproj, vecs, routerT, experts, eye, out):
    f32, f32r = mybir.dt.float32, mybir.dt.float32r
    ALU, ACT, AX = mybir.AluOpType, mybir.ActivationFunctionType, mybir.AxisListType
    ds = bass.ds
    es = ExitStack()
    with es:
        def sb(name, shape, dt=f32):
            return es.enter_context(nc.sbuf_tensor(name, shape, dt))

        def sem(name):
            return es.enter_context(nc.semaphore(name))

        x = sb("x", [P, CH, SEQS, PAD])
        ctx = sb("ctx", [P, CH, SEQS, STEPS])
        dx = sb("dx", [P, CH, SEQS, STEPS])
        rmix = sb("rmix", [P, CH, SEQS, STEPS])
        x2 = sb("x2", [P, CH, TOK])
        x2h = sb("x2h", [P, CH, TOK], f32r)
        x2l = sb("x2l", [P, CH, TOK], f32r)
        wp = sb("wp", [P, 4, CH, DIM])
        vec = sb("vec", [P, 11, CH])
        rw = sb("rw", [P, CH, EXPERTS])
        ident = sb("ident", [P, P])
        avg = sb("avg", [P, P])
        zero = sb("zero", [P, P], f32r)
        eps = sb("eps", [P, 1])
        kw = sb("kw", [P, CH])
        wk = sb("wk", [P, CH])
        w2n = sb("w2n", [P, CH])
        decay = sb("decay", [P, CH, UNIT_SEQS, PAD])

        class Unit:
            pass

        units = []
        for j in range(2):
            w = Unit()
            slot = [sb(f"slot{j}_{i}", [P, SEGS, PAD]) for i in range(7)]
            full = lambda i, slot=slot: slot[i][:, :, :].rearrange("p g s -> p (g s)")[:, 0:CH * UT].rearrange(
                "p (c t) -> p c t", c=CH)
            w.kvmix = [full(0), full(1)]
            w.e2, w.e1, w.e2v, w.den1, w.num1 = (full(i) for i in range(2, 7))
            w.z, w.sq = [full(0), full(3)], [full(1), full(4)]
            w.r0 = [full(4)[:, 0, :], full(5)[:, 0, :]]
            w.vr = [full(4)[:, 1, :], full(5)[:, 1, :]]
            w.o, w.o_step, w.k_o, w.k_oprev = slot[0], full(1), full(2), full(3)
            w.aa, w.ee, w.ev = full(4), full(5), full(6)
            w.pst, w.qst, w.den2, w.num2 = slot[0], slot[1], full(2), full(3)
            w.rd0, w.rdn = full(1), full(0)
            w.x1, w.a2, w.ek, w.ekv = (sb(f"{n}_{j}", [P, SEGS, PAD]) for n in ("x1", "a2", "ek", "ekv"))
            units.append(w)
        kvmix23 = [[sb(f"kvmix{u}_{i}", [P, CH, UT])[:, :, :] for i in range(2)] for u in (2, 3)]

        def unit(u):
            return units[u % 2]

        def kvmix(u, i):
            return units[u].kvmix[i] if u < 2 else kvmix23[u - 2][i]

        top = sb("top", [P, TH])
        ex = sb("ex", [P, TH, EXPERTS])
        zsum = sb("zsum", [P, TH])
        probs = sb("probs", [P, TH, EXPERTS])
        best = sb("best", [P, TH, TOPK])
        marked = sb("marked", [P, TH, EXPERTS])
        csum = sb("csum", [P, TH])
        gateT = sb("gateT", [EXPERTS, HT])
        gates = sb("gates", [P, HALVES, GROUPS, HT])

        raw = [sb(f"raw{i}", [P, 3 * DIM]) for i in range(2)]
        whi = [sb(f"whi{i}", [P, 3 * DIM], f32r) for i in range(SLOTS)]
        wlo = [sb(f"wlo{i}", [P, 3 * DIM], f32r) for i in range(SLOTS)]
        sg = [sb(f"sg{i}", [P, HT]) for i in range(2)]
        h = [sb(f"h{i}", [P, HT]) for i in range(2)]
        hh = [sb(f"hh{i}", [P, HT], f32r) for i in range(2)]
        hl = [sb(f"hl{i}", [P, HT], f32r) for i in range(2)]

        z3 = dx[:, :, :, :].rearrange("p c b s -> p c (b s)")
        sq3 = rmix[:, :, :, :].rearrange("p c b s -> p c (b s)")
        rows3 = ctx[:, :, :, :].rearrange("p c b s -> p c (b s)")
        r03, vr3 = rows3[:, 0, :], rows3[:, 1, :]

        ps = es.enter_context(nc.psum_tensor("ps", [P, 8, 512], f32))

        def bank(u, what):
            if u < 2:
                return 4 * u + {"k": 0, "v": 1, "r": 2, "o": 3, "ln0": 0, "ln1": 1}[what]
            return {"k": 2, "v": 3, "r": 2}[what] + 4 * (u - 2) if what in "kvr" else u

        def pc(b):
            return ps[:, b, :].rearrange("p (c t) -> p c t", c=CH)

        router_banks = [(6, 7), (3, 2)]
        parts3 = [(0, HT), (HT, HT + UT), (HT + UT, TOK)]
        mean3_bank, var3_bank = [0, 4, 5], [1, 6, 7]

        s_x = [sem(f"x_in{i}") for i in range(2)]
        s_ctx, s_small, s_wp = sem("ctx_in"), sem("small_in"), sem("wp_in")
        names = """consts pads zeros dx rmixed silu_r kvmixed k_proj v_proj r_proj kept_k kept_v kept_r relu_k e2 e1 e2v
            num1 den1 rden1 wkv y1 o_proj x1 o_scan o_step k_o k_oprev a2 ek ekv relu_x aa ee ev
            p_scan q_scan ap aq num2 den2 lnd rd0 gd rdn yn x2 x2h x2l
            logits top shifted ex zsum rz probs best marked chosen csum rcs gate gateT_ps gateT
            w_hi w_lo g u silu sw h hh hl down out z3 mean3 cen3 sq3 var3 lnv3 r03 r0sq3 vr3 rn3
            y3 sums""".split()
        s = {n: sem("s_" + n) for n in names}
        s_z, s_mean, s_cen, s_sq, s_var, s_lnv, s_r0, s_r0sq, s_vr, s_rn = (
            [sem(f"s_{n}{i}") for i in (1, 2)]
            for n in "z mean cen sq var lnv r0 r0sq vr rn".split())
        s_raw = [sem(f"raw{i}_in") for i in range(2)]
        s_gates = [sem(f"gates_in{g}") for g in range(GROUPS)]

        def need(eng, sm, n):
            if not isinstance(n, int) or n > 0:
                eng.wait_ge(sm, n)

        block = es.enter_context(nc.Block())

        @block.sync
        def _(sp):
            hs = SEQS // 2
            sp.wait_ge(s["pads"], 1)
            for c in range(CH):
                sp.dma_start(x[:, c, 0:hs, 1:PAD], xT[:, c, 0:hs, :]).then_inc(s_x[0], 16)
            sp.dma_start(wp[:, :, :, :], wproj).then_inc(s_wp, 16)
            for c in range(CH):
                sp.dma_start(x[:, c, hs:SEQS, 1:PAD], xT[:, c, hs:SEQS, :]).then_inc(s_x[1], 16)
            sp.dma_start(ctx[:, :, :, :], ctxT).then_inc(s_ctx, 16)
            for w in range(2):
                sp.dma_start(raw[w][:, :], experts[w]).then_inc(s_raw[w], 16)

            def refill(w, row):
                for i in range(2):
                    sp.wait_ge(s["w_hi"], w + i - 1)
                    sp.wait_ge(s["w_lo"], w + i - 1)
                    sp.dma_start(raw[i][:, :], experts[ds(row + i, 1)].rearrange("a p n -> (a p) n")
                                 ).then_inc(s_raw[i], 16)

            with sp.Fori(1, TILES // 2) as q:
                refill(2 * q, 2 * q)
            with sp.Fori(0, TILES // 2) as q:
                refill(2 * q + TILES, 2 * q)
            for k, (a, b) in enumerate(parts3):
                sp.wait_ge(s["y3"], k + 1)
                sp.dma_start(out[:, :, a:b], z3[:, :, a:b]).then_inc(s["out"], 16)
            sp.wait_ge(s["out"], 16 * len(parts3))

        @block.gpsimd
        def _(pool):
            nc.gpsimd.memset(x[:, :, :, 0:1], 0.0).then_inc(s["pads"], 1)
            for un in units:
                for t_ in (un.a2, un.ek, un.ekv):
                    nc.gpsimd.memset(t_[:, :, 0:1], 0.0).then_inc(s["pads"], 1)
            seg = lambda t_: t_.rearrange("p c (b s) -> p (c b) s", s=STEPS)

            def rest_w(w, i):
                pool.wait_ge(s["w_hi"], w + 1)
                nc.gpsimd.tensor_tensor(wlo[i % SLOTS][:, :], raw[i % 2][:, :],
                                        whi[i % SLOTS][:, :].bitcast(f32),
                                        ALU.subtract).then_inc(s["w_lo"], 1)

            def weigh1(u):
                un = unit(u)
                pool.wait_ge(s["num1"], SEGS * (u + 1))
                pool.wait_ge(s["rden1"], CH * (u + 1))
                nc.gpsimd.tensor_tensor(un.num1, un.num1, un.den1, ALU.mult).then_inc(s["wkv"], 1)

            def lead2(u):
                un = unit(u)
                pool.wait_ge(s["o_scan"], u + 1)
                nc.gpsimd.tensor_tensor(seg(un.k_oprev), un.x1[:, :, 1:PAD], un.o[:, :, 0:STEPS],
                                        ALU.subtract).then_inc(s["k_oprev"], 1)

            def values2(u):
                un = unit(u)
                cx = ctx[:, :, u * UNIT_SEQS:(u + 1) * UNIT_SEQS, :]
                v4 = lambda t_: t_.rearrange("p (c b) s -> p c b s", c=CH)
                pool.wait_ge(s["ek"], u + 1)
                nc.gpsimd.tensor_tensor(v4(un.ekv[:, :, 1:PAD]), v4(un.ek[:, :, 1:PAD]), cx,
                                        ALU.mult).then_inc(s["ekv"], 1)
                pool.wait_ge(s["ee"], u + 1)
                b4 = lambda t_: t_.rearrange("p c (b s) -> p c b s", s=STEPS)
                nc.gpsimd.tensor_tensor(b4(un.ev), b4(un.ee), cx, ALU.mult).then_inc(s["ev"], 1)

            def weigh(n, hf, j):
                if isinstance(n, int) and n % TILES < GROUPS:
                    pool.wait_ge(s_gates[j % GROUPS], 16 * (hf + 1))
                pool.wait_ge(s["silu"], n + 1)
                nc.gpsimd.tensor_tensor(sg[j % 2][:, :], sg[j % 2][:, :], gates[:, hf, j % GROUPS, :],
                                        ALU.mult).then_inc(s["sw"], 1)

            rest_w(0, 0)
            weigh1(0)
            rest_w(1, 1)
            pool.wait_ge(s_ctx, 16)
            lead2(0)
            lead2(1)
            values2(0)
            values2(1)

            def step(n, hf, j, ahead=True):
                weigh(n, hf, j)
                if ahead:
                    rest_w(n + 2, j + 2)

            for n in range(TILES):
                step(n, 0, n)
                if n == 9:
                    values2(2)
                if n == 11:
                    values2(3)

            for n in range(TILES, TILES + GROUPS):
                step(n, 1, n)
            with pool.Fori(TILES // GROUPS + 1, STEPS_ALL // GROUPS - 1) as q:
                for j in range(GROUPS):
                    step(GROUPS * q + j, 1, j)
            for n in range(STEPS_ALL - GROUPS, STEPS_ALL):
                step(n, 1, n, n + 2 < STEPS_ALL)

        @block.scalar
        def _(act):
            act.dma_start(vec[:, :, :], vecs).then_inc(s_small, 16)
            act.dma_start(rw[:, :, :], routerT).then_inc(s_small, 16)
            act.dma_start(ident[:, :], eye).then_inc(s_small, 16)
            seg2 = lambda t_, c: t_[:, UNIT_SEQS * c:UNIT_SEQS * (c + 1), 1:PAD]
            b2 = lambda t_, c: t_[:, c, :].rearrange("p (b s) -> p b s", s=STEPS)

            def silu_r(hf):
                act.wait_ge(s["rmixed"], CH * (hf + 1))
                v_ = rmix[:, :, hf * SEQS // 2:(hf + 1) * SEQS // 2, :]
                nc.scalar.activation(v_, v_, ACT.Silu).then_inc(s["silu_r"], 1)

            def relus1(u):
                un, kp = unit(u), pc(bank(u, "k"))
                act.wait_ge(s["k_proj"], u + 1)
                for c in range(CH):
                    nc.scalar.activation(un.e2[:, c, :], kp[:, c, :], ACT.Relu, bias=wk[:, c:c + 1],
                                         scale=-1.0).then_inc(s["relu_k"], 1)
                for c in range(CH):
                    nc.scalar.activation(un.e1[:, c, :], kp[:, c, :], ACT.Relu, bias=kw[:, c:c + 1],
                                         scale=1.0).then_inc(s["relu_k"], 1)

            def keep(u, what, bias, over):
                act.wait_ge(s[f"{what}_proj"], u + 1)
                for c in range(CH):
                    nc.scalar.activation(over[c], pc(bank(u, what))[:, c, :], ACT.Identity,
                                         bias=bias[c]).then_inc(s[f"kept_{what}"], 1)

            def keep_k(u):
                keep(u, "k", [kw[:, c:c + 1] for c in range(CH)], [kvmix(u, 0)[:, c, :] for c in range(CH)])

            def keep_v(u):
                keep(u, "v", [vec[:, BV, c:c + 1] for c in range(CH)],
                     [kvmix(u, 1)[:, c, :] for c in range(CH)])

            def keep_r(u):
                seqs = slice(u * UNIT_SEQS, (u + 1) * UNIT_SEQS)
                keep(u, "r", [vec[:, BR, c:c + 1] for c in range(CH)],
                     [rmix[:, c, seqs, :].rearrange("p b s -> p (b s)") for c in range(CH)])

            def exps1(u):
                un = unit(u)
                act.wait_ge(s["relu_k"], 2 * CH * u + CH)
                nc.scalar.activation(un.e2, un.e2, ACT.Exp, scale=-1.0).then_inc(s["e2"], 1)
                act.wait_ge(s["relu_k"], 2 * CH * (u + 1))
                for c in range(CH):
                    nc.scalar.activation(un.e1[:, c, :], un.e1[:, c, :], ACT.Exp, bias=w2n[:, c:c + 1],
                                         scale=-1.0).then_inc(s["e1"], 1)

            def exps2a(u):
                un = unit(u)
                act.wait_ge(s["o_step"], u + 1)
                for c in range(CH):
                    nc.scalar.activation(seg2(un.a2, c), b2(un.o_step, c), ACT.Exp,
                                         bias=vec[:, XW, c:c + 1]).then_inc(s["a2"], 1)
                act.wait_ge(s["k_o"], u + 1)
                nc.scalar.activation(un.ek[:, :, 1:PAD],
                                     un.k_o.rearrange("p c (b s) -> p (c b) s", s=STEPS),
                                     ACT.Exp).then_inc(s["ek"], 1)

            def exps2b(u):
                un = unit(u)
                act.wait_ge(s["relu_x"], 2 * CH * u + CH)
                nc.scalar.activation(un.ee, un.ee, ACT.Exp).then_inc(s["ee"], 1)
                act.wait_ge(s["relu_x"], 2 * CH * (u + 1))
                nc.scalar.activation(un.aa, un.aa, ACT.Exp, scale=-1.0).then_inc(s["aa"], 1)

            def first_rden2(u):
                un = unit(u)
                act.wait_ge(s["den2"], u + 1)
                nc.scalar.activation(un.rd0, un.den2, ACT.Ln).then_inc(s["lnd"], 1)
                act.wait_ge(s["lnd"], u + 1)
                nc.scalar.activation(un.rd0, un.rd0, ACT.Exp, scale=-1.0).then_inc(s["rd0"], 1)

            def square(n, u):
                un = unit(u)
                act.wait_ge(s_cen[n], u + 1)
                nc.scalar.activation(un.sq[n], un.z[n], ACT.Square).then_inc(s_sq[n], 1)

            def first_rstd(n, u):
                un = unit(u)
                act.wait_ge(s_var[n], u + 1)
                nc.scalar.activation(un.r0[n], ps[:, bank(u, f"ln{n}"), UT:2 * UT], ACT.Ln,
                                     bias=eps[:, :]).then_inc(s_lnv[n], 1)
                act.wait_ge(s_lnv[n], u + 1)
                nc.scalar.activation(un.r0[n], un.r0[n], ACT.Exp, scale=-0.5).then_inc(s_r0[n], 1)
                act.wait_ge(s_r0[n], u + 1)
                nc.scalar.activation(un.vr[n], un.r0[n], ACT.Square).then_inc(s_r0sq[n], 1)

            def upper_x2(u):
                act.wait_ge(s["x2"], u + 1)
                at = slice(u * UT, (u + 1) * UT)
                nc.scalar.activation(x2h[:, :, at], x2[:, :, at], ACT.Copy).then_inc(s["x2h"], 1)

            def router_exp(hf):
                act.wait_ge(s["shifted"], hf + 1)
                nc.scalar.activation(ex[:, :, :], ex[:, :, :], ACT.Exp).then_inc(s["ex"], 1)

            def router_out(hf):
                act.wait_ge(s["gateT_ps"], hf + 1)
                if hf:
                    for g in range(GROUPS):
                        act.wait_ge(s_gates[g], 16)
                nc.scalar.activation(gateT[:, :], ps[0:EXPERTS, router_banks[hf][1], :],
                                     ACT.Copy).then_inc(s["gateT"], 1)
                act.wait_ge(s["gateT"], hf + 1)
                for gr in range(GROUPS):
                    act.dma_start(gates[:, hf, gr, :],
                                  gateT[EG * gr:EG * (gr + 1), :].unsqueeze(1).to_broadcast(
                                      [EG, IG, HT])).then_inc(s_gates[gr], 16)

            def upper_w(w, i, raws):
                act.wait_ge(s_raw[i % 2], 16 * raws)
                need(act, s["down"], w - SLOTS + 1)
                nc.scalar.activation(whi[i % SLOTS][:, :], raw[i % 2][:, :], ACT.Copy).then_inc(s["w_hi"], 1)

            def silu(n, i):
                act.wait_ge(s["g"], n + 1)
                if not isinstance(n, int) or n >= 2:
                    act.wait_ge(s["h"], n - 1)
                nc.scalar.activation(sg[i][:, :], ps[:, 4 + 2 * i, :], ACT.Silu).then_inc(s["silu"], 1)

            def upper_h(n, i):
                act.wait_ge(s["h"], n + 1)
                need(act, s["down"], n - 1)
                nc.scalar.activation(hh[i][:, :], h[i][:, :], ACT.Copy).then_inc(s["hh"], 1)

            exp_ln = lambda: act.preload_act_table_set("natural_log_exp_and_others")
            silu_r(0)
            exp_ln()
            act.wait_ge(s["consts"], 4)
            for u in (0, 1):
                relus1(u)
                exps1(u)
            upper_w(0, 0, 1)
            upper_w(1, 1, 1)
            silu_r(1)
            exp_ln()
            for u in (0, 1):
                square(0, u)
            for u in (0, 1):
                first_rstd(0, u)
            keep_k(2)
            keep_k(3)
            for u in (0, 1):
                exps2a(u)
                exps2b(u)
            keep_v(2)
            keep_v(3)
            first_rden2(0)
            keep_r(2)
            first_rden2(1)
            keep_r(3)
            for u in (0, 1):
                square(1, u)
            for u in (0, 1):
                first_rstd(1, u)
            for u in (0, 1):
                upper_x2(u)
            exps1(2)
            router_exp(0)
            exps1(3)

            def step(n, j, raws, ahead=True, beside=None):
                silu(n, j % 2)
                if ahead:
                    upper_w(n + 2, j + 2, raws)
                if beside:
                    beside(n)
                upper_h(n, j % 2)

            def beside(n):
                if n == 0:
                    router_out(0)
                if n == 6:
                    square(0, 2)
                if n == 7:
                    exp_ln()
                    first_rstd(0, 2)
                if n == 8:
                    square(0, 3)
                if n == 9:
                    exp_ln()
                    first_rstd(0, 3)
                    exps2a(2)
                    exps2b(2)
                if n == 11:
                    exp_ln()
                    exps2a(3)
                    exps2b(3)
                if n == 13:
                    exp_ln()
                    first_rden2(2)
                if n == 15:
                    exp_ln()
                    first_rden2(3)
                if n == 17:
                    square(1, 2)
                if n == 18:
                    square(1, 3)
                    exp_ln()
                    first_rstd(1, 2)
                if n == 19:
                    upper_x2(2)
                    exp_ln()
                    first_rstd(1, 3)
                if n == 20:
                    upper_x2(3)
                if n == 21:
                    exp_ln()
                    router_exp(1)
                if n == 23:
                    router_out(1)

            for n in range(TILES):
                step(n, n, (n + 2) // 2 + 1, beside=beside)

            def step_b(q, j, beside=None):
                step(GROUPS * q + j, j, (GROUPS // 2) * q + j // 2 + 2, beside=beside)

            def rstd3(k):
                at, w = slice(*parts3[k]), parts3[k][1] - parts3[k][0]
                act.wait_ge(s["var3"], k + 1)
                nc.scalar.activation(r03[:, at], ps[:, var3_bank[k], 0:w], ACT.Ln,
                                     bias=eps[:, :]).then_inc(s["lnv3"], 1)
                act.wait_ge(s["lnv3"], k + 1)
                nc.scalar.activation(r03[:, at], r03[:, at], ACT.Exp, scale=-0.5).then_inc(s["r03"], 1)
                act.wait_ge(s["r03"], k + 1)
                nc.scalar.activation(vr3[:, at], r03[:, at], ACT.Square).then_inc(s["r0sq3"], 1)

            def square3(k):
                at = slice(*parts3[k])
                act.wait_ge(s["cen3"], k + 1)
                nc.scalar.activation(sq3[:, :, at], z3[:, :, at], ACT.Square).then_inc(s["sq3"], 1)

            def beside3(n):
                if n == TILES + 5:
                    square3(0)
                if n == TILES + 7:
                    exp_ln()
                    rstd3(0)

            for j in range(GROUPS):
                step_b(TILES // GROUPS, j, beside=beside3)
            with act.Fori(TILES // GROUPS + 1, STEPS_ALL // GROUPS - 1) as q:
                for j in range(GROUPS):
                    step_b(q, j)
            for n in range(STEPS_ALL - GROUPS, STEPS_ALL):
                step(n, n, (n + 2) // 2 + 1, n + 2 < STEPS_ALL)
            exp_ln()
            square3(1)
            square3(2)
            rstd3(1)
            rstd3(2)

        @block.vector
        def _(dve):
            hs = SEQS // 2
            bs = lambda t_: t_.rearrange("p (b s) -> p b s", s=STEPS)
            seg = lambda t_: t_.rearrange("p c (b s) -> p (c b) s", s=STEPS)
            line = lambda t_: t_[:, :, :].rearrange("p g s -> p (g s)")

            def diff(hf):
                sl = slice(hf * hs, (hf + 1) * hs)
                dve.wait_ge(s_x[hf], 16 * CH)
                nc.vector.tensor_tensor(dx[:, :, sl, :], x[:, :, sl, 1:PAD], x[:, :, sl, 0:STEPS],
                                        ALU.subtract).then_inc(s["dx"], 1)
                dve.wait_ge(s["dx"], hf + 1)

            def mix_r(hf):
                sl = slice(hf * hs, (hf + 1) * hs)
                for c in range(CH):
                    nc.vector.scalar_tensor_tensor(rmix[:, c, sl, :], dx[:, c, sl, :], vec[:, TMR, c:c + 1],
                                                   x[:, c, sl, 0:STEPS], ALU.mult,
                                                   ALU.add).then_inc(s["rmixed"], 1)

            def mix_kv(u):
                seqs = slice(u * UNIT_SEQS, (u + 1) * UNIT_SEQS)
                for n, tm in enumerate((TMK, TMV)):
                    for c in range(CH):
                        nc.vector.scalar_tensor_tensor(
                            bs(kvmix(u, n)[:, c, :]), dx[:, c, seqs, :], vec[:, tm, c:c + 1],
                            x[:, c, seqs, 0:STEPS], ALU.mult, ALU.add).then_inc(s["kvmixed"], 1)

            segs = [(c, slice(b * STEPS, (b + 1) * STEPS)) for c in range(CH) for b in range(UNIT_SEQS)]

            def relus1(u):
                un = unit(u)
                dve.wait_ge(s["kept_k"], CH * (u - 1))
                nc.vector.tensor_scalar(un.e2, kvmix(u, 0), -1.0, 0.0, ALU.mult,
                                        ALU.max).then_inc(s["relu_k"], CH)
                nc.vector.tensor_scalar(un.e1, kvmix(u, 0), 0.0, None, ALU.max).then_inc(s["relu_k"], CH)

            def scans1(u):
                un, vp = unit(u), pc(bank(u, "v"))
                dve.wait_ge(s["e2"], u + 1)
                dve.wait_ge(s["e1"], CH * (u + 1))
                for c, at in segs:
                    nc.vector.tensor_tensor_scan(un.den1[:, c, at], un.e1[:, c, at], un.e2[:, c, at], 0.0,
                                                 ALU.mult, ALU.add).then_inc(s["den1"], 1)
                if u < 2:
                    dve.wait_ge(s["v_proj"], u + 1)
                    for c in range(CH):
                        nc.vector.scalar_tensor_tensor(un.e2v[:, c, :], vp[:, c, :], vec[:, BV, c:c + 1],
                                                       un.e2[:, c, :], ALU.add, ALU.mult).then_inc(s["e2v"], 1)
                else:
                    dve.wait_ge(s["kept_v"], CH * (u - 1))
                    nc.vector.tensor_tensor(un.e2v, kvmix(u, 1), un.e2, ALU.mult).then_inc(s["e2v"], CH)
                for c, at in segs:
                    dve.wait_ge(s["e2v"], CH * u + c + 1)
                    nc.vector.tensor_tensor_scan(un.num1[:, c, at], un.e1[:, c, at], un.e2v[:, c, at], 0.0,
                                                 ALU.mult, ALU.add).then_inc(s["num1"], 1)

            def invert1(u, c):
                un = unit(u)
                dve.wait_ge(s["den1"], SEGS * u + UNIT_SEQS * (c + 1))
                nc.vector.reciprocal(un.den1[:, c, :], un.den1[:, c, :]).then_inc(s["rden1"], 1)

            def weigh1(u):
                un = unit(u)
                dve.wait_ge(s["num1"], SEGS * (u + 1))
                dve.wait_ge(s["rden1"], CH * (u + 1))
                nc.vector.tensor_tensor(un.num1, un.num1, un.den1, ALU.mult).then_inc(s["wkv"], 1)

            def times_r(u):
                un, rp = unit(u), pc(bank(u, "r"))
                dve.wait_ge(s["wkv"], u + 1)
                if u < 2:
                    dve.wait_ge(s["r_proj"], u + 1)
                    for c in range(CH):
                        nc.vector.scalar_tensor_tensor(un.num1[:, c, :], rp[:, c, :], vec[:, BR, c:c + 1],
                                                       un.num1[:, c, :], ALU.add, ALU.mult).then_inc(s["y1"], 1)
                else:
                    dve.wait_ge(s["kept_r"], CH * (u - 1))
                    seqs = slice(u * UNIT_SEQS, (u + 1) * UNIT_SEQS)
                    b4 = lambda t_: t_.rearrange("p c (b s) -> p c b s", s=STEPS)
                    nc.vector.tensor_tensor(b4(un.num1), b4(un.num1), rmix[:, :, seqs, :],
                                            ALU.mult).then_inc(s["y1"], CH)

            def residual1(u):
                un, op = unit(u), pc(bank(u, "o"))
                dve.wait_ge(s["o_proj"], u + 1)
                seqs = slice(u * UNIT_SEQS, (u + 1) * UNIT_SEQS)
                for c in range(CH):
                    nc.vector.scalar_tensor_tensor(bs(un.z[0][:, c, :]), bs(op[:, c, :]),
                                                   vec[:, BO, c:c + 1], x[:, c, seqs, 1:PAD], ALU.add,
                                                   ALU.add).then_inc(s_z[0], 1)

            def center(n, u):
                un = unit(u)
                dve.wait_ge(s_mean[n], u + 1)
                mean = ps[:, bank(u, f"ln{n}"), 0:UT].unsqueeze(1).to_broadcast([P, CH, UT])
                nc.vector.tensor_tensor(un.z[n], un.z[n], mean, ALU.subtract).then_inc(s_cen[n], 1)

            def newton_rstd(n, u):
                un = unit(u)
                dve.wait_ge(s_r0sq[n], u + 1)
                nc.vector.scalar_tensor_tensor(un.vr[n], ps[:, bank(u, f"ln{n}"), UT:2 * UT], EPS, un.vr[n],
                                               ALU.add, ALU.mult).then_inc(s_vr[n], 1)
                dve.wait_ge(s_vr[n], u + 1)
                nc.vector.scalar_tensor_tensor(un.vr[n], un.vr[n], -3.0, un.r0[n],
                                               ALU.add, ALU.mult).then_inc(s_rn[n], 1)
                dve.wait_ge(s_rn[n], u + 1)

            def norm1(u):
                newton_rstd(0, u)
                un = unit(u)
                for c in range(CH):
                    nc.vector.scalar_tensor_tensor(un.x1[:, UNIT_SEQS * c:UNIT_SEQS * (c + 1), 1:PAD],
                                                   bs(un.z[0][:, c, :]), -0.5, bs(un.vr[0]), ALU.mult,
                                                   ALU.mult).then_inc(s["x1"], 1)

            def norm2(u):
                newton_rstd(1, u)
                un = unit(u)
                nc.vector.scalar_tensor_tensor(x2[:, :, u * UT:(u + 1) * UT], un.z[1], -0.5,
                                               un.vr[1].unsqueeze(1).to_broadcast([P, CH, UT]),
                                               ALU.mult, ALU.mult).then_inc(s["x2"], 1)

            def rest_x2(u):
                dve.wait_ge(s["x2h"], u + 1)
                at = slice(u * UT, (u + 1) * UT)
                nc.vector.tensor_tensor(x2l[:, :, at], x2[:, :, at], x2h[:, :, at].bitcast(f32),
                                        ALU.subtract).then_inc(s["x2l"], 1)

            def max_scan(u):
                un = unit(u)
                dve.wait_ge(s["x1"], CH * (u + 1))
                nc.vector.tensor_tensor_scan(line(un.o), decay[:, :, :, :].rearrange("p c b s -> p (c b s)"),
                                             line(un.x1), FAR, ALU.add, ALU.max).then_inc(s["o_scan"], 1)

            def against_o(u):
                un = unit(u)
                dve.wait_ge(s["o_scan"], u + 1)
                nc.vector.tensor_tensor(seg(un.o_step), un.o[:, :, 0:STEPS], un.o[:, :, 1:PAD],
                                        ALU.subtract).then_inc(s["o_step"], 1)
                nc.vector.tensor_tensor(seg(un.k_o), un.x1[:, :, 1:PAD], un.o[:, :, 1:PAD],
                                        ALU.subtract).then_inc(s["k_o"], 1)

            def lead2(u):
                un = unit(u)
                dve.wait_ge(s["o_scan"], u + 1)
                nc.vector.tensor_tensor(seg(un.k_oprev), un.x1[:, :, 1:PAD], un.o[:, :, 0:STEPS],
                                        ALU.subtract).then_inc(s["k_oprev"], 1)

            def limit2(u):
                un = unit(u)
                dve.wait_ge(s["k_oprev"], u + 1)
                for c in range(CH):
                    nc.vector.tensor_scalar(un.ee[:, c, :], un.k_oprev[:, c, :], vec[:, XU, c:c + 1], 0.0,
                                            ALU.add, ALU.min).then_inc(s["relu_x"], 1)
                for c in range(CH):
                    nc.vector.tensor_scalar(un.aa[:, c, :], un.k_oprev[:, c, :], vec[:, XU, c:c + 1], 0.0,
                                            ALU.add, ALU.max).then_inc(s["relu_x"], 1)

            def scans2(u):
                un = unit(u)
                dve.wait_ge(s["a2"], CH * (u + 1))
                dve.wait_ge(s["ek"], u + 1)
                nc.vector.tensor_tensor_scan(line(un.qst), line(un.a2), line(un.ek), 0.0, ALU.mult,
                                             ALU.add).then_inc(s["q_scan"], 1)
                dve.wait_ge(s["k_oprev"], u + 1)
                dve.wait_ge(s["ekv"], u + 1)
                nc.vector.tensor_tensor_scan(line(un.pst), line(un.a2), line(un.ekv), 0.0, ALU.mult,
                                             ALU.add).then_inc(s["p_scan"], 1)

            def outputs2(u):
                un = unit(u)
                dve.wait_ge(s["aa"], u + 1)
                dve.wait_ge(s["q_scan"], u + 1)
                nc.vector.tensor_tensor(seg(un.den2), seg(un.aa), un.qst[:, :, 0:STEPS], ALU.mult).then_inc(s["aq"], 1)

            def outputs2b(u):
                un = unit(u)
                dve.wait_ge(s["p_scan"], u + 1)
                nc.vector.tensor_tensor(seg(un.num2), seg(un.aa), un.pst[:, :, 0:STEPS], ALU.mult).then_inc(s["ap"], 1)
                dve.wait_ge(s["aq"], u + 1)
                nc.vector.tensor_tensor(un.den2, un.den2, un.ee, ALU.add).then_inc(s["den2"], 1)
                dve.wait_ge(s["ap"], u + 1)
                dve.wait_ge(s["ev"], u + 1)
                nc.vector.tensor_tensor(un.num2, un.num2, un.ev, ALU.add).then_inc(s["num2"], 1)

            def residual2(u):
                un = unit(u)
                dve.wait_ge(s["rd0"], u + 1)
                nc.vector.tensor_tensor(un.rdn, un.den2, un.rd0, ALU.mult).then_inc(s["gd"], 1)
                dve.wait_ge(s["gd"], u + 1)
                nc.vector.scalar_tensor_tensor(un.rdn, un.rdn, -2.0, un.rd0, ALU.add,
                                               ALU.mult).then_inc(s["rdn"], 1)
                dve.wait_ge(s["rdn"], u + 1)
                dve.wait_ge(s["num2"], u + 1)
                nc.vector.tensor_tensor(un.num2, un.num2, un.rdn, ALU.mult).then_inc(s["yn"], 1)
                dve.wait_ge(s["yn"], u + 1)
                nc.vector.scalar_tensor_tensor(seg(un.z[1]), seg(un.num2), -1.0, un.x1[:, :, 1:PAD],
                                               ALU.mult, ALU.add).then_inc(s_z[1], 1)

            wide = lambda t_: t_[:, :].unsqueeze(2).to_broadcast([P, TH, EXPERTS])

            def router_a(hf):
                logits = ps[:, router_banks[hf][0], 0:TH * EXPERTS].rearrange("p (t e) -> p t e", t=TH)
                dve.wait_ge(s["logits"], hf + 1)
                nc.vector.tensor_reduce(top[:, :], logits, AX.X, ALU.max).then_inc(s["top"], 1)
                dve.wait_ge(s["top"], hf + 1)
                nc.vector.tensor_tensor(ex[:, :, :], logits, wide(top), ALU.subtract).then_inc(s["shifted"], 1)

            def router_b(hf):
                dve.wait_ge(s["ex"], hf + 1)
                nc.vector.tensor_reduce(zsum[:, :], ex[:, :, :], AX.X, ALU.add).then_inc(s["zsum"], 1)
                dve.wait_ge(s["zsum"], hf + 1)
                nc.vector.reciprocal(zsum[:, :], zsum[:, :]).then_inc(s["rz"], 1)
                dve.wait_ge(s["rz"], hf + 1)
                nc.vector.tensor_tensor(probs[:, :, :], ex[:, :, :], wide(zsum), ALU.mult).then_inc(s["probs"], 1)
                dve.wait_ge(s["probs"], hf + 1)
                for t in range(TH):
                    nc.vector.max(best[:, t, :], probs[:, t, :]).then_inc(s["best"], 1)
                for t in range(TH):
                    dve.wait_ge(s["best"], TH * hf + t + 1)
                    nc.vector.match_replace(marked[:, t, :], best[:, t, :], probs[:, t, :],
                                            -1.0).then_inc(s["marked"], 1)
                dve.wait_ge(s["marked"], TH * (hf + 1))
                nc.vector.scalar_tensor_tensor(probs[:, :, :], marked[:, :, :], 0.0, probs[:, :, :],
                                               ALU.is_lt, ALU.mult).then_inc(s["chosen"], 1)
                dve.wait_ge(s["chosen"], hf + 1)
                nc.vector.tensor_reduce(csum[:, :], probs[:, :, :], AX.X, ALU.add).then_inc(s["csum"], 1)
                dve.wait_ge(s["csum"], hf + 1)
                nc.vector.reciprocal(csum[:, :], csum[:, :]).then_inc(s["rcs"], 1)
                dve.wait_ge(s["rcs"], hf + 1)
                nc.vector.tensor_tensor(probs[:, :, :], probs[:, :, :], wide(csum), ALU.mult).then_inc(s["gate"], 1)

            def hidden(n, i):
                dve.wait_ge(s["sw"], n + 1)
                dve.wait_ge(s["u"], n + 1)
                nc.vector.tensor_tensor(h[i][:, :], ps[:, 5 + 2 * i, :], sg[i][:, :],
                                        ALU.mult).then_inc(s["h"], 1)

            def rest_h(n, i):
                dve.wait_ge(s["hh"], n + 1)
                need(dve, s["down"], n - 1)
                nc.vector.tensor_tensor(hl[i][:, :], h[i][:, :], hh[i][:, :].bitcast(f32),
                                        ALU.subtract).then_inc(s["hl"], 1)

            nc.vector.memset(avg[:, :], 1.0 / DIM).then_inc(s["consts"], 1)
            nc.vector.memset(eps[:, :], EPS).then_inc(s["zeros"], 1)
            nc.vector.memset(decay[:, :, :, :], 0.0).then_inc(s["zeros"], 1)
            for un in units:
                nc.vector.memset(un.x1[:, :, 0:1], FAR).then_inc(s["zeros"], 1)
            nc.vector.memset(zero[:, :].bitcast(f32), 0.0).then_inc(s["zeros"], 1)
            ZEROS = 3 + len(units)
            dve.wait_ge(s_small, 16 * 3)
            v = lambda i: vec[:, i, :]
            nc.vector.tensor_tensor(kw[:, :], v(BK), v(U_), ALU.add).then_inc(s["zeros"], 1)
            nc.vector.tensor_scalar(w2n[:, :], v(W_), -2.0, None, ALU.mult).then_inc(s["consts"], 1)
            dve.wait_ge(s["zeros"], ZEROS + 1)
            nc.vector.tensor_tensor(wk[:, :], v(W_), kw[:, :], ALU.subtract).then_inc(s["consts"], 1)
            dve.wait_ge(s["consts"], 3)
            nc.vector.tensor_scalar(kw[:, :], wk[:, :], -1.0, None, ALU.mult).then_inc(s["consts"], 1)
            diff(0)
            mix_kv(0)
            mix_kv(1)
            mix_r(0)
            for c in range(CH):
                nc.vector.tensor_scalar(decay[:, c, :, :], decay[:, c, :, :], vec[:, XW, c:c + 1], None,
                                        ALU.add).then_inc(s["zeros"], 1)
            dve.wait_ge(s["zeros"], ZEROS + 1 + CH)
            nc.vector.memset(decay[:, :, :, 0:1], FAR).then_inc(s["zeros"], 1)
            scans1(0)
            invert1(0, 0)
            invert1(0, 1)
            scans1(1)
            invert1(1, 0)
            invert1(1, 1)
            times_r(0)
            weigh1(1)
            times_r(1)
            diff(1)
            mix_r(1)
            mix_kv(2)
            residual1(0)
            mix_kv(3)
            residual1(1)
            center(0, 0)
            center(0, 1)
            dve.wait_ge(s["zeros"], ZEROS + 2 + CH)
            dve.wait_ge(s["pads"], 7)
            for u in (0, 1):
                norm1(u)
                max_scan(u)
                against_o(u)
            for u in (0, 1):
                limit2(u)
            for u in (0, 1):
                scans2(u)
                outputs2(u)
                outputs2b(u)
            for u in (0, 1):
                residual2(u)
            for u in (0, 1):
                center(1, u)
            for u in (0, 1):
                norm2(u)
            for u in (0, 1):
                rest_x2(u)
            relus1(2)
            router_a(0)
            relus1(3)
            router_b(0)
            scans1(2)
            scans1(3)
            invert1(2, 0)

            def step(n, i):
                hidden(n, i)
                rest_h(n, i)

            for n in range(TILES):
                step(n, n % 2)
                if n == 0:
                    invert1(2, 1)
                    weigh1(2)
                if n == 1:
                    times_r(2)
                    invert1(3, 0)
                if n == 2:
                    invert1(3, 1)
                    weigh1(3)
                if n == 3:
                    times_r(3)
                    residual1(2)
                if n == 5:
                    center(0, 2)
                    residual1(3)
                if n == 7:
                    center(0, 3)
                    norm1(2)
                    max_scan(2)
                if n == 8:
                    against_o(2)
                    lead2(2)
                    limit2(2)
                if n == 9:
                    norm1(3)
                    max_scan(3)
                if n == 10:
                    against_o(3)
                    lead2(3)
                    limit2(3)
                if n == 11:
                    scans2(2)
                    outputs2(2)
                    outputs2b(2)
                if n == 13:
                    scans2(3)
                    outputs2(3)
                    outputs2b(3)
                if n == 14:
                    residual2(2)
                if n == 15:
                    residual2(3)
                if n == 16:
                    center(1, 2)
                if n == 17:
                    center(1, 3)
                if n == 18:
                    norm2(2)
                if n == 19:
                    norm2(3)
                    rest_x2(2)
                if n == 20:
                    rest_x2(3)
                    router_a(1)
                if n == 21:
                    router_b(1)

            def residual3(k):
                at, w = slice(*parts3[k]), parts3[k][1] - parts3[k][0]
                a, hf = parts3[k][0] % HT, parts3[k][0] // HT
                dve.wait_ge(s["sums"], hf + 1)
                nc.vector.tensor_tensor(z3[:, :, at], ps[:, 2 * hf:2 * hf + 2, a:a + w], x2[:, :, at],
                                        ALU.add).then_inc(s["z3"], 1)

            def center3(k):
                at, w = slice(*parts3[k]), parts3[k][1] - parts3[k][0]
                dve.wait_ge(s["mean3"], k + 1)
                nc.vector.tensor_tensor(z3[:, :, at], z3[:, :, at],
                                        ps[:, mean3_bank[k], 0:w].unsqueeze(1).to_broadcast([P, CH, w]),
                                        ALU.subtract).then_inc(s["cen3"], 1)

            def norm3(k):
                at, w = slice(*parts3[k]), parts3[k][1] - parts3[k][0]
                dve.wait_ge(s["r0sq3"], k + 1)
                nc.vector.scalar_tensor_tensor(vr3[:, at], ps[:, var3_bank[k], 0:w], EPS, vr3[:, at],
                                               ALU.add, ALU.mult).then_inc(s["vr3"], 1)
                dve.wait_ge(s["vr3"], k + 1)
                nc.vector.scalar_tensor_tensor(vr3[:, at], vr3[:, at], -3.0, r03[:, at], ALU.add,
                                               ALU.mult).then_inc(s["rn3"], 1)
                dve.wait_ge(s["rn3"], k + 1)
                nc.vector.scalar_tensor_tensor(z3[:, :, at], z3[:, :, at], -0.5,
                                               vr3[:, at].unsqueeze(1).to_broadcast([P, CH, w]),
                                               ALU.mult, ALU.mult).then_inc(s["y3"], 1)

            for j in range(GROUPS):
                step(TILES + j, j % 2)
                if j == 2:
                    residual3(0)
                if j == 4:
                    center3(0)
                if j == 7:
                    norm3(0)
            with dve.Fori(TILES // GROUPS + 1, STEPS_ALL // GROUPS) as q:
                for j in range(GROUPS):
                    step(GROUPS * q + j, j % 2)
            for f in (residual3, center3, norm3):
                for k in (1, 2):
                    f(k)

        @block.tensor
        def _(pe):
            mm = nc.tensor.matmul

            def project(b, which, src):
                for mo in range(CH):
                    for k in range(CH):
                        last = mm(pc(b)[:, mo, :], wp[:, which, k, mo * P:(mo + 1) * P], src(k),
                                  start=(k == 0), stop=(k == CH - 1))
                return last

            def project_k(u):
                pe.wait_ge(s["kvmixed"], 2 * CH * u + CH)
                project(bank(u, "k"), K_, lambda k: kvmix(u, 0)[:, k, :]).then_inc(s["k_proj"], 1)

            def project_v(u):
                pe.wait_ge(s["kvmixed"], 2 * CH * (u + 1))
                project(bank(u, "v"), V_, lambda k: kvmix(u, 1)[:, k, :]).then_inc(s["v_proj"], 1)

            def project_r(u):
                pe.wait_ge(s["silu_r"], u // 2 + 1)
                seqs = slice(u * UNIT_SEQS, (u + 1) * UNIT_SEQS)
                project(bank(u, "r"), R_, lambda k: rmix[:, k, seqs, :]).then_inc(s["r_proj"], 1)

            def project_out(u):
                pe.wait_ge(s["y1"], CH * (u + 1))
                project(bank(u, "o"), O_, lambda k: unit(u).num1[:, k, :]).then_inc(s["o_proj"], 1)

            def mean(n, u):
                pe.wait_ge(s_z[n], (CH if n == 0 else 1) * (u + 1))
                for k in range(CH):
                    last = mm(ps[:, bank(u, f"ln{n}"), 0:UT], avg[:, :], unit(u).z[n][:, k, :],
                              start=(k == 0), stop=(k == CH - 1))
                last.then_inc(s_mean[n], 1)

            def variance(n, u):
                pe.wait_ge(s_sq[n], u + 1)
                for k in range(CH):
                    last = mm(ps[:, bank(u, f"ln{n}"), UT:2 * UT], avg[:, :], unit(u).sq[n][:, k, :],
                              start=(k == 0), stop=(k == CH - 1))
                last.then_inc(s_var[n], 1)

            def route(hf):
                pe.wait_ge(s["x2"], 2 * (hf + 1))
                for t in range(TH):
                    a = (TH * hf + t) * P
                    for k in range(CH):
                        last = mm(ps[:, router_banks[hf][0], t * EXPERTS:(t + 1) * EXPERTS], x2[:, k, a:a + P],
                                  rw[:, k, :], start=(k == 0), stop=(k == CH - 1))
                last.then_inc(s["logits"], 1)

            def turn_gates(hf):
                pe.wait_ge(s["gate"], hf + 1)
                for t in range(TH):
                    last = nc.tensor.transpose(ps[0:EXPERTS, router_banks[hf][1], t * P:(t + 1) * P],
                                               probs[:, t, :], ident[:, :])
                last.then_inc(s["gateT_ps"], 1)

            def up(which, n, j, hf):
                i, w_ = j % 2, j % SLOTS
                if which == 0:
                    pe.wait_ge(s["w_hi"], n + 1)
                need_ = s["silu" if which == 0 else "h"]
                if not isinstance(n, int) or n >= 2:
                    pe.wait_ge(need_, n - 1)
                parts = [(k, whi, x_) for k in range(CH) for x_ in (x2h, x2l)]
                parts += [(k, wlo, x2h) for k in range(CH)]
                for m, (k, part, x_) in enumerate(parts):
                    a = which * DIM + k * P
                    if part is wlo and which == 0:
                        pe.wait_ge(s["w_lo"], n + 1)
                    last = mm(ps[:, 4 + 2 * i + which, :], part[w_][:, a:a + P],
                              x_[:, k, hf * HT:(hf + 1) * HT], start=(m == 0), stop=(m == len(parts) - 1))
                last.then_inc(s["g" if which == 0 else "u"], 1)

            def down(n, j, hf):
                i, w_ = j % 2, j % SLOTS
                pe.wait_ge(s["hh"], n + 1)
                pe.wait_ge(s["hl"], n + 1)
                for mo in range(CH):
                    a = 2 * DIM + mo * P
                    for w__, h_ in ((whi, hh), (whi, hl), (wlo, hh)):
                        last = mm(ps[:, 2 * hf + mo, :], w__[w_][:, a:a + P], h_[i][:, :],
                                  start=False, stop=False)
                last.then_inc(s["down"], 1)

            def sums(hf, **flag):
                for mo in range(CH):
                    last = mm(ps[:, 2 * hf + mo, :], zero[:, :], x2h[:, 0, hf * HT:(hf + 1) * HT], **flag)
                return last

            pe.wait_ge(s_wp, 16)
            pe.wait_ge(s["consts"], 1)
            for u in (0, 1):
                project_k(u)
                project_v(u)
            for u in (0, 1):
                project_r(u)
            for u in (0, 1):
                project_out(u)
            project_k(2)
            project_k(3)
            for u in (0, 1):
                mean(0, u)
            for u in (0, 1):
                variance(0, u)
            project_v(2)
            project_v(3)
            pe.wait_ge(s["kept_k"], 2 * CH)
            project_r(2)
            project_r(3)
            for u in (0, 1):
                mean(1, u)
            for u in (0, 1):
                variance(1, u)

            def step(n, j, hf):
                up(0, n, j, hf)
                down(n - 2, j - 2, hf)
                up(1, n, j, hf)

            pe.wait_ge(s["kept_r"], 2 * CH)
            route(0)
            pe.wait_ge(s["x2h"], 2)
            pe.wait_ge(s["x2l"], 2)
            up(0, 0, 0, 0)
            up(1, 0, 0, 0)
            pe.wait_ge(s["zeros"], 5)
            sums(0, start=True, stop=False)
            turn_gates(0)
            pe.wait_ge(s["gateT"], 1)
            up(0, 1, 1, 0)
            up(1, 1, 1, 0)
            for n in range(2, TILES):
                step(n, n, 0)
                if n == 3:
                    project_out(2)
                if n == 5:
                    mean(0, 2)
                    project_out(3)
                if n == 6:
                    variance(0, 2)
                if n == 7:
                    mean(0, 3)
                if n == 8:
                    variance(0, 3)
                if n == 16:
                    mean(1, 2)
                if n == 17:
                    variance(1, 2)
                    mean(1, 3)
                if n == 18:
                    variance(1, 3)
                if n == 20:
                    route(1)
                if n == 22:
                    turn_gates(1)
            pe.wait_ge(s["gateT"], 2)

            pe.wait_ge(s["x2h"], 4)
            pe.wait_ge(s["x2l"], 4)
            sums(1, start=True, stop=False)
            for j in range(2):
                up(0, TILES + j, j, 1)
                down(TILES - 2 + j, TILES - 2 + j, 0)
                up(1, TILES + j, j, 1)
            sums(0, start=False, stop=True).then_inc(s["sums"], 1)
            def average3(k, of, bank_, sm):
                (a, b) = parts3[k]
                for c in range(CH):
                    last = mm(ps[:, bank_[k], 0:b - a], avg[:, :], of[:, c, a:b],
                              start=(c == 0), stop=(c == CH - 1))
                last.then_inc(sm, 1)

            def mean3(k):
                pe.wait_ge(s["z3"], k + 1)
                average3(k, z3, mean3_bank, s["mean3"])

            def variance3(k):
                pe.wait_ge(s["sq3"], k + 1)
                average3(k, sq3, var3_bank, s["var3"])

            for j in range(2, GROUPS):
                step(TILES + j, j, 1)
                if j == 4:
                    mean3(0)
                if j == 6:
                    variance3(0)
            with pe.Fori(TILES // GROUPS + 1, STEPS_ALL // GROUPS) as q:
                for j in range(GROUPS):
                    step(GROUPS * q + j, GROUPS + j, 1)
            for n in range(STEPS_ALL - 2, STEPS_ALL):
                down(n, n, 1)
            sums(1, start=False, stop=True).then_inc(s["sums"], 1)
            for f in (mean3, variance3):
                for k in (1, 2):
                    f(k)


def kernel(**inputs):
    import numpy as np
    import concourse.bacc as bacc
    from concourse.bass_utils import run_bass_kernel_spmd as run

    a = {n: np.asarray(v) for n, v in inputs.items()}
    at = {n[len("L0_attn_"):]: v for n, v in a.items() if n.startswith("L0_attn_")}

    def channels(t):
        return t.reshape(SEQS, STEPS, CH, P).transpose(3, 2, 0, 1)

    def rows(w):
        return w.T.reshape(CH, P, -1).transpose(1, 0, 2)

    vectors = [at["bk"], at["bv"], at["br"], at["bo"], at["tmk"], at["tmv"], at["tmr"], at["u"],
               at["w"], a["L0_xattn_w"], a["L0_xattn_u"]]

    def up_rows(w):
        w = w.reshape(GROUPS, EG, CH, P, INNER // IG, IG).transpose(4, 0, 3, 2, 1, 5)
        return w.reshape(TILES, P, CH * P)

    down_rows = a["L0_ffn_w_down"].reshape(GROUPS, EG, INNER // IG, IG, DIM).transpose(
        2, 0, 1, 3, 4)
    arrays = {
        "xT": channels(a["x"]),
        "ctxT": channels(a["ctx_2048"]),
        "wproj": np.stack([rows(at[n]) for n in ("Wk", "Wv", "Wr", "Wo")], axis=1),
        "vecs": np.stack([v.reshape(CH, P).T for v in vectors], axis=1),
        "routerT": rows(a["L0_ffn_router_w"]),
        "experts": np.concatenate([up_rows(a["L0_ffn_w_gate"]), up_rows(a["L0_ffn_w_up"]),
                                   down_rows.reshape(TILES, P, DIM)], axis=2),
        "eye": np.eye(P, dtype=np.float32),
    }
    arrays = {n: np.ascontiguousarray(v) for n, v in arrays.items()}
    nc = bacc.Bacc("TRN2", target_bir_lowering=False, num_devices=1)
    args = [nc.dram_tensor(f"in_{n}", v.shape, mybir.dt.from_np(v.dtype), kind="ExternalInput").ap()
            for n, v in arrays.items()]
    out = nc.dram_tensor("out", (P, CH, TOK), mybir.dt.float32, kind="ExternalOutput").ap()
    build(nc, *args, out)
    r = run(nc, [{f"in_{n}": v for n, v in arrays.items()}], core_ids=[0])
    y = np.asarray(r.results[0]["out"])
    return y.transpose(2, 1, 0).reshape(SEQS, STEPS, DIM)
```

```python
import concourse.bass as bass
from concourse import mybir
from contextlib import ExitStack

P = 128
SEQS, STEPS, DIM = 8, 128, 256
TOK = SEQS * STEPS
CH = DIM // P
UNIT_SEQS = 2
UNITS = SEQS // UNIT_SEQS
UT = UNIT_SEQS * STEPS
PAD = STEPS + 1
SEGS = CH * UNIT_SEQS
EXPERTS, INNER, TOPK = 32, 96, 8
EG, IG = 4, 32
GROUPS = EXPERTS // EG
TILES = INNER // IG * GROUPS
SLOTS = 4
HALVES = 2
HT = TOK // HALVES
STEPS_ALL = HALVES * TILES
TH = HT // P
EPS = 1e-5
FAR = -1e38
K_, V_, R_, O_ = range(4)
BK, BV, BR, BO, TMK, TMV, TMR, U_, W_, XW, XU = range(11)


def build(nc, xT, ctxT, wproj, vecs, routerT, experts, eye, out):
    f32, f32r = mybir.dt.float32, mybir.dt.float32r
    ALU, ACT, AX = mybir.AluOpType, mybir.ActivationFunctionType, mybir.AxisListType
    ds = bass.ds
    es = ExitStack()
    with es:
        def sb(name, shape, dt=f32):
            return es.enter_context(nc.sbuf_tensor(name, shape, dt))

        def sem(name):
            return es.enter_context(nc.semaphore(name))

        x = sb("x", [P, CH, SEQS, PAD])
        ctx = sb("ctx", [P, CH, SEQS, STEPS])
        dx = sb("dx", [P, CH, SEQS, STEPS])
        rmix = sb("rmix", [P, CH, SEQS, STEPS])
        x2 = sb("x2", [P, CH, TOK])
        x2h = sb("x2h", [P, CH, TOK], f32r)
        x2l = sb("x2l", [P, CH, TOK], f32r)
        wp = sb("wp", [P, 4, CH, DIM])
        vec = sb("vec", [P, 11, CH])
        rw = sb("rw", [P, CH, EXPERTS])
        ident = sb("ident", [P, P])
        avg = sb("avg", [P, P])
        zero = sb("zero", [P, P], f32r)
        eps = sb("eps", [P, 1])
        kw = sb("kw", [P, CH])
        wk = sb("wk", [P, CH])
        xun = sb("xun", [P, CH])
        w2n = sb("w2n", [P, CH])
        decay = sb("decay", [P, CH, UNIT_SEQS, PAD])

        class Unit:
            pass

        units = []
        for j in range(2):
            w = Unit()
            slot = [sb(f"slot{j}_{i}", [P, SEGS, PAD]) for i in range(7)]
            full = lambda i, slot=slot: slot[i][:, :, :].rearrange("p g s -> p (g s)")[:, 0:CH * UT].rearrange(
                "p (c t) -> p c t", c=CH)
            w.kvmix = [full(0), full(1)]
            w.e2, w.e1, w.e2v, w.den1, w.num1 = (full(i) for i in range(2, 7))
            w.z, w.sq = [full(0), full(3)], [full(1), full(4)]
            w.r0 = [full(4)[:, 0, :], full(5)[:, 0, :]]
            w.vr = [full(4)[:, 1, :], full(5)[:, 1, :]]
            w.o, w.o_step, w.k_o, w.k_oprev = slot[0], full(1), full(2), full(3)
            w.aa, w.ee, w.ev = full(4), full(5), full(6)
            w.pst, w.qst, w.den2, w.num2 = slot[0], slot[1], full(2), full(3)
            w.rd0, w.rdn = full(1), full(0)
            w.x1, w.a2, w.ek, w.ekv = (sb(f"{n}_{j}", [P, SEGS, PAD]) for n in ("x1", "a2", "ek", "ekv"))
            units.append(w)
        kvmix23 = [[sb(f"kvmix{u}_{i}", [P, CH, UT])[:, :, :] for i in range(2)] for u in (2, 3)]

        def unit(u):
            return units[u % 2]

        def kvmix(u, i):
            return units[u].kvmix[i] if u < 2 else kvmix23[u - 2][i]

        top = sb("top", [P, TH])
        ex = sb("ex", [P, TH, EXPERTS])
        zsum = sb("zsum", [P, TH])
        probs = sb("probs", [P, TH, EXPERTS])
        best = sb("best", [P, TH, TOPK])
        marked = sb("marked", [P, TH, EXPERTS])
        csum = sb("csum", [P, TH])
        gateT = sb("gateT", [EXPERTS, HT])
        gates = sb("gates", [P, HALVES, GROUPS, HT])

        raw = [sb(f"raw{i}", [P, 3 * DIM]) for i in range(2)]
        whi = [sb(f"whi{i}", [P, 3 * DIM], f32r) for i in range(SLOTS)]
        wlo = [sb(f"wlo{i}", [P, 3 * DIM], f32r) for i in range(SLOTS)]
        sg = [sb(f"sg{i}", [P, HT]) for i in range(2)]
        h = [sb(f"h{i}", [P, HT]) for i in range(2)]
        hh = [sb(f"hh{i}", [P, HT], f32r) for i in range(2)]
        hl = [sb(f"hl{i}", [P, HT], f32r) for i in range(2)]

        z3 = dx[:, :, :, :].rearrange("p c b s -> p c (b s)")
        sq3 = rmix[:, :, :, :].rearrange("p c b s -> p c (b s)")
        rows3 = ctx[:, :, :, :].rearrange("p c b s -> p c (b s)")
        r03, vr3 = rows3[:, 0, :], rows3[:, 1, :]

        ps = es.enter_context(nc.psum_tensor("ps", [P, 8, 512], f32))

        def bank(u, what):
            if u < 2:
                return 4 * u + {"k": 0, "v": 1, "r": 2, "o": 3, "ln0": 0, "ln1": 1}[what]
            return {"k": 2, "v": 3, "r": 2}[what] + 4 * (u - 2) if what in "kvr" else u

        def pc(b):
            return ps[:, b, :].rearrange("p (c t) -> p c t", c=CH)

        parts3 = [(0, HT), (HT, HT + UT), (HT + UT, TOK)]
        mean3_bank, var3_bank = [0, 4, 5], [1, 6, 7]

        s_x = [sem(f"x_in{i}") for i in range(2)]
        s_ctx, s_vec, s_small = sem("ctx_in"), sem("vec_in"), sem("small_in")
        s_wp = [sem(f"wp{i}_in") for i in range(2)]
        names = """consts pads zeros dx rmixed silu_r kvmixed k_proj v_proj r_proj kept_k kept_v
            kept_r relu_k e2 e1 e2v num1 den1 rden1 wkv y1 o_proj x1 o_scan o_step k_o k_oprev a2 ek ekv relu_x aa ee ev
            p_scan q_scan ap aq num2 den2 lnd rd0 gd rdn yn x2 x2h x2l
            logits top shifted ex zsum rz probs best marked chosen csum rcs gate gateT_ps gateT
            w_hi w_lo g u silu sw h hh hl down out z3 mean3 cen3 sq3 var3 lnv3 r03 r0sq3 vr3 rn3
            y3 sums""".split()
        s = {n: sem("s_" + n) for n in names}
        s_z, s_mean, s_cen, s_sq, s_var, s_lnv, s_r0, s_r0sq, s_vr, s_rn = (
            [sem(f"s_{n}{i}") for i in (1, 2)]
            for n in "z mean cen sq var lnv r0 r0sq vr rn".split())
        s_raw = [sem(f"raw{i}_in") for i in range(2)]
        s_gates = [sem(f"gates_in{g}") for g in range(GROUPS)]

        def need(eng, sm, n):
            if not isinstance(n, int) or n > 0:
                eng.wait_ge(sm, n)

        block = es.enter_context(nc.Block())

        @block.sync
        def _(sp):
            hs = SEQS // 2
            sp.wait_ge(s["pads"], 1)
            for c in range(CH):
                sp.dma_start(x[:, c, 0:hs, 1:PAD], xT[:, c, 0:hs, :]).then_inc(s_x[0], 16)
            sp.dma_start(wp[:, K_, :, :], wproj[:, K_, :, :]).then_inc(s_wp[0], 16)
            sp.dma_start(wp[:, K_ + 1:, :, :], wproj[:, K_ + 1:, :, :]).then_inc(s_wp[1], 16)
            for c in range(CH):
                sp.dma_start(x[:, c, hs:SEQS, 1:PAD], xT[:, c, hs:SEQS, :]).then_inc(s_x[1], 16)
            sp.dma_start(ctx[:, :, :, :], ctxT).then_inc(s_ctx, 16)
            for w in range(2):
                sp.dma_start(raw[w][:, :], experts[w]).then_inc(s_raw[w], 16)

            def refill(w, row):
                for i in range(2):
                    sp.wait_ge(s["w_hi"], w + i - 1)
                    sp.wait_ge(s["w_lo"], w + i - 1)
                    sp.dma_start(raw[i][:, :], experts[ds(row + i, 1)].rearrange("a p n -> (a p) n")
                                 ).then_inc(s_raw[i], 16)

            with sp.Fori(1, TILES // 2) as q:
                refill(2 * q, 2 * q)
            with sp.Fori(0, TILES // 2) as q:
                refill(2 * q + TILES, 2 * q)
            for k, (a, b) in enumerate(parts3):
                sp.wait_ge(s["y3"], k + 1)
                sp.dma_start(out[:, :, a:b], z3[:, :, a:b]).then_inc(s["out"], 16)
            sp.wait_ge(s["out"], 16 * len(parts3))

        @block.gpsimd
        def _(pool):
            nc.gpsimd.memset(x[:, :, :, 0:1], 0.0).then_inc(s["pads"], 1)
            for un in units:
                for t_ in (un.a2, un.ek, un.ekv):
                    nc.gpsimd.memset(t_[:, :, 0:1], 0.0).then_inc(s["pads"], 1)
            seg = lambda t_: t_.rearrange("p c (b s) -> p (c b) s", s=STEPS)

            def rest_w(w, i):
                pool.wait_ge(s["w_hi"], w + 1)
                nc.gpsimd.tensor_tensor(wlo[i % SLOTS][:, :], raw[i % 2][:, :],
                                        whi[i % SLOTS][:, :].bitcast(f32),
                                        ALU.subtract).then_inc(s["w_lo"], 1)

            def weigh1(u):
                un = unit(u)
                pool.wait_ge(s["num1"], SEGS * (u + 1))
                pool.wait_ge(s["rden1"], CH * (u + 1))
                nc.gpsimd.tensor_tensor(un.num1, un.num1, un.den1, ALU.mult).then_inc(s["wkv"], 1)

            def against_o_before(u):
                un = unit(u)
                pool.wait_ge(s["o_scan"], u + 1)
                nc.gpsimd.tensor_tensor(seg(un.k_oprev), un.x1[:, :, 1:PAD], un.o[:, :, 0:STEPS],
                                        ALU.subtract).then_inc(s["k_oprev"], 1)

            def numerator2(u):
                un = unit(u)
                pool.wait_ge(s["p_scan"], u + 1)
                pool.wait_ge(s["aa"], u + 1)
                nc.gpsimd.tensor_tensor(seg(un.num2), seg(un.aa), un.pst[:, :, 0:STEPS],
                                        ALU.mult).then_inc(s["ap"], 1)
                pool.wait_ge(s["ap"], u + 1)
                pool.wait_ge(s["ev"], u + 1)
                nc.gpsimd.tensor_tensor(un.num2, un.num2, un.ev, ALU.add).then_inc(s["num2"], 1)

            def value_ek(u):
                un = unit(u)
                cx = ctx[:, :, u * UNIT_SEQS:(u + 1) * UNIT_SEQS, :]
                v4 = lambda t_: t_.rearrange("p (c b) s -> p c b s", c=CH)
                if u == 0:
                    pool.wait_ge(s_ctx, 16)
                pool.wait_ge(s["ek"], u + 1)
                nc.gpsimd.tensor_tensor(v4(un.ekv[:, :, 1:PAD]), v4(un.ek[:, :, 1:PAD]), cx,
                                        ALU.mult).then_inc(s["ekv"], 1)

            def value_ee(u):
                un = unit(u)
                cx = ctx[:, :, u * UNIT_SEQS:(u + 1) * UNIT_SEQS, :]
                pool.wait_ge(s["ee"], u + 1)
                b4 = lambda t_: t_.rearrange("p c (b s) -> p c b s", s=STEPS)
                nc.gpsimd.tensor_tensor(b4(un.ev), b4(un.ee), cx, ALU.mult).then_inc(s["ev"], 1)

            def weigh(n):
                i = n % 2
                if n < GROUPS:
                    pool.wait_ge(s_gates[n], 16)
                pool.wait_ge(s["silu"], n + 1)
                nc.gpsimd.tensor_tensor(sg[i][:, :], sg[i][:, :], gates[:, 0, n % GROUPS, :],
                                        ALU.mult).then_inc(s["sw"], 1)

            weigh1(0)
            against_o_before(0)
            value_ek(0)
            against_o_before(1)
            value_ek(1)
            value_ee(0)
            value_ee(1)
            numerator2(1)
            rest_w(0, 0)
            rest_w(1, 1)
            rest_w(2, 2)

            for n in range(TILES):
                weigh(n)
                if n > 0:
                    rest_w(n + 2, n + 2)
                if n == 6:
                    value_ee(2)
                if n == 10:
                    value_ek(2)
                if n == 11:
                    value_ek(3)
                if n == 12:
                    value_ee(3)

            for n in range(TILES, TILES + GROUPS):
                rest_w(n + 2, n + 2)
            with pool.Fori(TILES // GROUPS + 1, STEPS_ALL // GROUPS - 1) as q:
                for j in range(GROUPS):
                    rest_w(GROUPS * q + j + 2, j + 2)
            for n in range(STEPS_ALL - GROUPS, STEPS_ALL - 2):
                rest_w(n + 2, n + 2)

        @block.scalar
        def _(act):
            act.dma_start(vec[:, :, :], vecs).then_inc(s_vec, 16)
            act.dma_start(rw[:, :, :], routerT).then_inc(s_small, 16)
            act.dma_start(ident[:, :], eye).then_inc(s_small, 16)
            seg2 = lambda t_, c: t_[:, UNIT_SEQS * c:UNIT_SEQS * (c + 1), 1:PAD]
            b2 = lambda t_, c: t_[:, c, :].rearrange("p (b s) -> p b s", s=STEPS)

            def silu_r(hf):
                act.wait_ge(s["rmixed"], CH * (hf + 1))
                v_ = rmix[:, :, hf * SEQS // 2:(hf + 1) * SEQS // 2, :]
                nc.scalar.activation(v_, v_, ACT.Silu).then_inc(s["silu_r"], 1)

            def relus1(u):
                un, kp = unit(u), pc(bank(u, "k"))
                act.wait_ge(s["k_proj"], u + 1)
                for c in range(CH):
                    nc.scalar.activation(un.e2[:, c, :], kp[:, c, :], ACT.Relu, bias=wk[:, c:c + 1],
                                         scale=-1.0).then_inc(s["relu_k"], 1)
                for c in range(CH):
                    nc.scalar.activation(un.e1[:, c, :], kp[:, c, :], ACT.Relu, bias=kw[:, c:c + 1],
                                         scale=1.0).then_inc(s["relu_k"], 1)

            def keep(u, what, bias, over):
                act.wait_ge(s[f"{what}_proj"], u + 1)
                for c in range(CH):
                    nc.scalar.activation(over[c], pc(bank(u, what))[:, c, :], ACT.Identity,
                                         bias=bias[c]).then_inc(s[f"kept_{what}"], 1)

            def keep_k(u):
                keep(u, "k", [kw[:, c:c + 1] for c in range(CH)], [kvmix(u, 0)[:, c, :] for c in range(CH)])

            def keep_v(u):
                keep(u, "v", [vec[:, BV, c:c + 1] for c in range(CH)],
                     [kvmix(u, 1)[:, c, :] for c in range(CH)])

            def keep_r(u):
                seqs = slice(u * UNIT_SEQS, (u + 1) * UNIT_SEQS)
                keep(u, "r", [vec[:, BR, c:c + 1] for c in range(CH)],
                     [rmix[:, c, seqs, :].rearrange("p b s -> p (b s)") for c in range(CH)])

            def exps1(u):
                un = unit(u)
                act.wait_ge(s["relu_k"], 2 * CH * u + CH)
                nc.scalar.activation(un.e2, un.e2, ACT.Exp, scale=-1.0).then_inc(s["e2"], 1)
                act.wait_ge(s["relu_k"], 2 * CH * (u + 1))
                for c in range(CH):
                    nc.scalar.activation(un.e1[:, c, :], un.e1[:, c, :], ACT.Exp, bias=w2n[:, c:c + 1],
                                         scale=-1.0).then_inc(s["e1"], 1)

            def exps2a(u):
                un = unit(u)
                act.wait_ge(s["o_step"], u + 1)
                for c in range(CH):
                    nc.scalar.activation(seg2(un.a2, c), b2(un.o_step, c), ACT.Exp,
                                         bias=vec[:, XW, c:c + 1]).then_inc(s["a2"], 1)
                act.wait_ge(s["k_o"], u + 1)
                nc.scalar.activation(un.ek[:, :, 1:PAD],
                                     un.k_o.rearrange("p c (b s) -> p (c b) s", s=STEPS),
                                     ACT.Exp).then_inc(s["ek"], 1)

            def relus2(u):
                un = unit(u)
                act.wait_ge(s["k_oprev"], u + 1)
                for c in range(CH):
                    nc.scalar.activation(un.ee[:, c, :], un.k_oprev[:, c, :], ACT.Relu, scale=-1.0,
                                         bias=xun[:, c:c + 1]).then_inc(s["relu_x"], 1)
                for c in range(CH):
                    nc.scalar.activation(un.aa[:, c, :], un.k_oprev[:, c, :], ACT.Relu,
                                         bias=vec[:, XU, c:c + 1]).then_inc(s["relu_x"], 1)

            def exps2b(u):
                un = unit(u)
                act.wait_ge(s["relu_x"], 2 * CH * u + CH)
                nc.scalar.activation(un.ee, un.ee, ACT.Exp, scale=-1.0 if u < 2 else 1.0).then_inc(s["ee"], 1)
                act.wait_ge(s["relu_x"], 2 * CH * (u + 1))
                nc.scalar.activation(un.aa, un.aa, ACT.Exp, scale=-1.0).then_inc(s["aa"], 1)

            def first_rden2(u):
                un = unit(u)
                act.wait_ge(s["den2"], u + 1)
                nc.scalar.activation(un.rd0, un.den2, ACT.Ln).then_inc(s["lnd"], 1)
                act.wait_ge(s["lnd"], u + 1)
                nc.scalar.activation(un.rd0, un.rd0, ACT.Exp, scale=-1.0).then_inc(s["rd0"], 1)

            def square(n, u):
                un = unit(u)
                act.wait_ge(s_cen[n], u + 1)
                nc.scalar.activation(un.sq[n], un.z[n], ACT.Square).then_inc(s_sq[n], 1)

            def first_rstd(n, u):
                un = unit(u)
                act.wait_ge(s_var[n], u + 1)
                nc.scalar.activation(un.r0[n], ps[:, bank(u, f"ln{n}"), UT:2 * UT], ACT.Ln,
                                     bias=eps[:, :]).then_inc(s_lnv[n], 1)
                act.wait_ge(s_lnv[n], u + 1)
                nc.scalar.activation(un.r0[n], un.r0[n], ACT.Exp, scale=-0.5).then_inc(s_r0[n], 1)
                act.wait_ge(s_r0[n], u + 1)
                nc.scalar.activation(un.vr[n], un.r0[n], ACT.Square).then_inc(s_r0sq[n], 1)

            def upper_x2(u):
                act.wait_ge(s["x2"], u + 1)
                at = slice(u * UT, (u + 1) * UT)
                nc.scalar.activation(x2h[:, :, at], x2[:, :, at], ACT.Copy).then_inc(s["x2h"], 1)

            def router_exp(hf):
                act.wait_ge(s["shifted"], hf + 1)
                nc.scalar.activation(ex[:, :, :], ex[:, :, :], ACT.Exp).then_inc(s["ex"], 1)

            def router_out(hf):
                act.wait_ge(s["gateT_ps"], hf + 1)
                if hf:
                    for g in range(GROUPS):
                        act.wait_ge(s_gates[g], 16)
                nc.scalar.activation(gateT[:, :], ps[0:EXPERTS, 2, :],
                                     ACT.Copy).then_inc(s["gateT"], 1)
                act.wait_ge(s["gateT"], hf + 1)
                for gr in range(GROUPS):
                    act.dma_start(gates[:, hf, gr, :],
                                  gateT[EG * gr:EG * (gr + 1), :].unsqueeze(1).to_broadcast(
                                      [EG, IG, HT])).then_inc(s_gates[gr], 16)

            def upper_w(w, i, raws):
                act.wait_ge(s_raw[i % 2], 16 * raws)
                need(act, s["down"], w - SLOTS + 1)
                nc.scalar.activation(whi[i % SLOTS][:, :], raw[i % 2][:, :], ACT.Copy).then_inc(s["w_hi"], 1)

            def silu(n, i):
                act.wait_ge(s["g"], n + 1)
                if not isinstance(n, int) or n >= 2:
                    act.wait_ge(s["h"], n - 1)
                nc.scalar.activation(sg[i][:, :], ps[:, 4 + 2 * i, :], ACT.Silu).then_inc(s["silu"], 1)

            def upper_h(n, i):
                act.wait_ge(s["h"], n + 1)
                need(act, s["down"], n - 1)
                nc.scalar.activation(hh[i][:, :], h[i][:, :], ACT.Copy).then_inc(s["hh"], 1)

            def exp_ln():
                act.preload_act_table_set("natural_log_exp_and_others")

            act.wait_ge(s["consts"], 5)
            exp_ln()
            relus1(0)
            exps1(0)
            silu_r(0)
            exp_ln()
            relus1(1)
            exps1(1)
            silu_r(1)
            square(0, 0)
            upper_w(0, 0, 1)
            exp_ln()
            first_rstd(0, 0)
            square(0, 1)
            first_rstd(0, 1)
            exps2a(0)
            relus2(0)
            exps2b(0)
            exps2a(1)
            keep_k(2)
            relus2(1)
            first_rden2(0)
            exps2b(1)
            upper_w(1, 1, 1)
            first_rden2(1)
            square(1, 0)
            keep_v(2)
            keep_k(3)
            first_rstd(1, 0)
            square(1, 1)
            keep_r(2)
            first_rstd(1, 1)
            upper_x2(0)
            exps1(2)
            upper_x2(1)
            upper_w(2, 2, 2)
            router_exp(0)
            exps1(3)
            keep_v(3)

            def step(n, j, raws, ahead=True, beside=None):
                silu(n, j % 2)
                if ahead:
                    upper_w(n + 2, j + 2, raws)
                if beside:
                    beside(n)
                upper_h(n, j % 2)

            def beside(n):
                if n == 0:
                    keep_r(3)
                    router_out(0)
                if n == 4:
                    square(0, 2)
                if n == 5:
                    exp_ln()
                    first_rstd(0, 2)
                if n == 6:
                    square(0, 3)
                    exp_ln()
                    first_rstd(0, 3)
                    exps2a(2)
                    exps2b(2)
                if n == 11:
                    exp_ln()
                    first_rden2(2)
                    exps2a(3)
                if n == 12:
                    exp_ln()
                    exps2b(3)
                if n == 15:
                    exp_ln()
                    first_rden2(3)
                if n == 16:
                    square(1, 2)
                if n == 17:
                    square(1, 3)
                if n == 18:
                    exp_ln()
                    first_rstd(1, 2)
                    first_rstd(1, 3)
                if n == 19:
                    upper_x2(2)
                if n == 20:
                    exp_ln()
                    router_exp(1)
                if n == 21:
                    upper_x2(3)
                if n == 22:
                    router_out(1)

            for n in range(TILES):
                step(n, n, (n + 2) // 2 + 1, n > 0, beside)

            def step_b(q, j, beside=None):
                step(GROUPS * q + j, j, (GROUPS // 2) * q + j // 2 + 2, beside=beside)

            def rstd3(k):
                at, w = slice(*parts3[k]), parts3[k][1] - parts3[k][0]
                act.wait_ge(s["var3"], k + 1)
                nc.scalar.activation(r03[:, at], ps[:, var3_bank[k], 0:w], ACT.Ln,
                                     bias=eps[:, :]).then_inc(s["lnv3"], 1)
                act.wait_ge(s["lnv3"], k + 1)
                nc.scalar.activation(r03[:, at], r03[:, at], ACT.Exp, scale=-0.5).then_inc(s["r03"], 1)
                act.wait_ge(s["r03"], k + 1)
                nc.scalar.activation(vr3[:, at], r03[:, at], ACT.Square).then_inc(s["r0sq3"], 1)

            def square3(k):
                at = slice(*parts3[k])
                act.wait_ge(s["cen3"], k + 1)
                nc.scalar.activation(sq3[:, :, at], z3[:, :, at], ACT.Square).then_inc(s["sq3"], 1)

            def beside3(n):
                if n == TILES + 5:
                    square3(0)
                if n == TILES + 7:
                    exp_ln()
                    rstd3(0)

            for j in range(GROUPS):
                step_b(TILES // GROUPS, j, beside=beside3)
            with act.Fori(TILES // GROUPS + 1, STEPS_ALL // GROUPS - 1) as q:
                for j in range(GROUPS):
                    step_b(q, j)
            for n in range(STEPS_ALL - GROUPS, STEPS_ALL):
                step(n, n, (n + 2) // 2 + 1, n + 2 < STEPS_ALL)
            exp_ln()
            square3(1)
            square3(2)
            rstd3(1)
            rstd3(2)

        @block.vector
        def _(dve):
            hs = SEQS // 2
            bs = lambda t_: t_.rearrange("p (b s) -> p b s", s=STEPS)
            seg = lambda t_: t_.rearrange("p c (b s) -> p (c b) s", s=STEPS)
            line = lambda t_: t_[:, :, :].rearrange("p g s -> p (g s)")

            def diff(hf):
                sl = slice(hf * hs, (hf + 1) * hs)
                dve.wait_ge(s_x[hf], 16 * CH)
                nc.vector.tensor_tensor(dx[:, :, sl, :], x[:, :, sl, 1:PAD], x[:, :, sl, 0:STEPS],
                                        ALU.subtract).then_inc(s["dx"], 1)
                dve.wait_ge(s["dx"], hf + 1)

            def mix_r(hf):
                sl = slice(hf * hs, (hf + 1) * hs)
                for c in range(CH):
                    nc.vector.scalar_tensor_tensor(rmix[:, c, sl, :], dx[:, c, sl, :], vec[:, TMR, c:c + 1],
                                                   x[:, c, sl, 0:STEPS], ALU.mult,
                                                   ALU.add).then_inc(s["rmixed"], 1)

            def mix_kv(u):
                seqs = slice(u * UNIT_SEQS, (u + 1) * UNIT_SEQS)
                for n, tm in enumerate((TMK, TMV)):
                    for c in range(CH):
                        nc.vector.scalar_tensor_tensor(
                            bs(kvmix(u, n)[:, c, :]), dx[:, c, seqs, :], vec[:, tm, c:c + 1],
                            x[:, c, seqs, 0:STEPS], ALU.mult, ALU.add).then_inc(s["kvmixed"], 1)

            segs = [(c, slice(b * STEPS, (b + 1) * STEPS)) for c in range(CH) for b in range(UNIT_SEQS)]

            def relus1(u):
                un = unit(u)
                dve.wait_ge(s["kept_k"], CH * (u - 1))
                dve.wait_ge(s["x2"], u - 1)
                nc.vector.tensor_scalar(un.e2, kvmix(u, 0), -1.0, 0.0, ALU.mult,
                                        ALU.max).then_inc(s["relu_k"], CH)
                nc.vector.tensor_scalar(un.e1, kvmix(u, 0), 0.0, None, ALU.max).then_inc(s["relu_k"], CH)

            def scans1(u):
                un, vp = unit(u), pc(bank(u, "v"))
                dve.wait_ge(s["e2"], u + 1)
                dve.wait_ge(s["e1"], CH * (u + 1))
                for c, at in segs:
                    nc.vector.tensor_tensor_scan(un.den1[:, c, at], un.e1[:, c, at], un.e2[:, c, at], 0.0,
                                                 ALU.mult, ALU.add).then_inc(s["den1"], 1)
                if u < 2:
                    dve.wait_ge(s["v_proj"], u + 1)
                    for c in range(CH):
                        nc.vector.scalar_tensor_tensor(un.e2v[:, c, :], vp[:, c, :], vec[:, BV, c:c + 1],
                                                       un.e2[:, c, :], ALU.add, ALU.mult).then_inc(s["e2v"], 1)
                else:
                    dve.wait_ge(s["kept_v"], CH * (u - 1))
                    nc.vector.tensor_tensor(un.e2v, kvmix(u, 1), un.e2, ALU.mult).then_inc(s["e2v"], CH)
                for c, at in segs:
                    dve.wait_ge(s["e2v"], CH * u + c + 1)
                    nc.vector.tensor_tensor_scan(un.num1[:, c, at], un.e1[:, c, at], un.e2v[:, c, at], 0.0,
                                                 ALU.mult, ALU.add).then_inc(s["num1"], 1)

            def invert1(u, c):
                un = unit(u)
                dve.wait_ge(s["den1"], SEGS * u + UNIT_SEQS * (c + 1))
                nc.vector.reciprocal(un.den1[:, c, :], un.den1[:, c, :]).then_inc(s["rden1"], 1)

            def weigh1(u):
                un = unit(u)
                dve.wait_ge(s["num1"], SEGS * (u + 1))
                dve.wait_ge(s["rden1"], CH * (u + 1))
                nc.vector.tensor_tensor(un.num1, un.num1, un.den1, ALU.mult).then_inc(s["wkv"], 1)

            def times_r(u):
                un, rp = unit(u), pc(bank(u, "r"))
                dve.wait_ge(s["wkv"], u + 1)
                if u < 2:
                    dve.wait_ge(s["r_proj"], u + 1)
                    for c in range(CH):
                        nc.vector.scalar_tensor_tensor(un.num1[:, c, :], rp[:, c, :], vec[:, BR, c:c + 1],
                                                       un.num1[:, c, :], ALU.add, ALU.mult).then_inc(s["y1"], 1)
                else:
                    dve.wait_ge(s["kept_r"], CH * (u - 1))
                    seqs = slice(u * UNIT_SEQS, (u + 1) * UNIT_SEQS)
                    b4 = lambda t_: t_.rearrange("p c (b s) -> p c b s", s=STEPS)
                    nc.vector.tensor_tensor(b4(un.num1), b4(un.num1), rmix[:, :, seqs, :],
                                            ALU.mult).then_inc(s["y1"], CH)

            def residual1(u):
                un, op = unit(u), pc(bank(u, "o"))
                dve.wait_ge(s["o_proj"], u + 1)
                seqs = slice(u * UNIT_SEQS, (u + 1) * UNIT_SEQS)
                for c in range(CH):
                    nc.vector.scalar_tensor_tensor(bs(un.z[0][:, c, :]), bs(op[:, c, :]),
                                                   vec[:, BO, c:c + 1], x[:, c, seqs, 1:PAD], ALU.add,
                                                   ALU.add).then_inc(s_z[0], 1)

            def center(n, u):
                un = unit(u)
                dve.wait_ge(s_mean[n], u + 1)
                mean = ps[:, bank(u, f"ln{n}"), 0:UT].unsqueeze(1).to_broadcast([P, CH, UT])
                nc.vector.tensor_tensor(un.z[n], un.z[n], mean, ALU.subtract).then_inc(s_cen[n], 1)

            def newton_rstd(n, u):
                un = unit(u)
                dve.wait_ge(s_r0sq[n], u + 1)
                nc.vector.scalar_tensor_tensor(un.vr[n], ps[:, bank(u, f"ln{n}"), UT:2 * UT], EPS, un.vr[n],
                                               ALU.add, ALU.mult).then_inc(s_vr[n], 1)
                dve.wait_ge(s_vr[n], u + 1)
                nc.vector.scalar_tensor_tensor(un.vr[n], un.vr[n], -3.0, un.r0[n],
                                               ALU.add, ALU.mult).then_inc(s_rn[n], 1)
                dve.wait_ge(s_rn[n], u + 1)

            def norm1(u):
                newton_rstd(0, u)
                un = unit(u)
                for c in range(CH):
                    nc.vector.scalar_tensor_tensor(un.x1[:, UNIT_SEQS * c:UNIT_SEQS * (c + 1), 1:PAD],
                                                   bs(un.z[0][:, c, :]), -0.5, bs(un.vr[0]), ALU.mult,
                                                   ALU.mult).then_inc(s["x1"], 1)

            def norm2(u):
                newton_rstd(1, u)
                un = unit(u)
                nc.vector.scalar_tensor_tensor(x2[:, :, u * UT:(u + 1) * UT], un.z[1], -0.5,
                                               un.vr[1].unsqueeze(1).to_broadcast([P, CH, UT]),
                                               ALU.mult, ALU.mult).then_inc(s["x2"], 1)

            def rest_x2(u):
                dve.wait_ge(s["x2h"], u + 1)
                at = slice(u * UT, (u + 1) * UT)
                nc.vector.tensor_tensor(x2l[:, :, at], x2[:, :, at], x2h[:, :, at].bitcast(f32),
                                        ALU.subtract).then_inc(s["x2l"], 1)

            def set_decay():
                for c in range(CH):
                    nc.vector.tensor_scalar(decay[:, c, :, :], decay[:, c, :, :], vec[:, XW, c:c + 1], None,
                                            ALU.add).then_inc(s["zeros"], 1)
                dve.wait_ge(s["zeros"], ZEROS + 1 + CH)
                nc.vector.memset(decay[:, :, :, 0:1], FAR).then_inc(s["zeros"], 1)

            def max_scan(u):
                un = unit(u)
                if u == 0:
                    dve.wait_ge(s["zeros"], ZEROS + 2 + CH)
                    dve.wait_ge(s["pads"], 7)
                dve.wait_ge(s["x1"], CH * (u + 1))
                nc.vector.tensor_tensor_scan(line(un.o), decay[:, :, :, :].rearrange("p c b s -> p (c b s)"),
                                             line(un.x1), FAR, ALU.add, ALU.max).then_inc(s["o_scan"], 1)

            def step_of_o(u):
                un = unit(u)
                dve.wait_ge(s["o_scan"], u + 1)
                nc.vector.tensor_tensor(seg(un.o_step), un.o[:, :, 0:STEPS], un.o[:, :, 1:PAD],
                                        ALU.subtract).then_inc(s["o_step"], 1)

            def against_o(u):
                un = unit(u)
                dve.wait_ge(s["o_scan"], u + 1)
                nc.vector.tensor_tensor(seg(un.k_o), un.x1[:, :, 1:PAD], un.o[:, :, 1:PAD],
                                        ALU.subtract).then_inc(s["k_o"], 1)

            def against_o_before(u):
                un = unit(u)
                dve.wait_ge(s["o_scan"], u + 1)
                nc.vector.tensor_tensor(seg(un.k_oprev), un.x1[:, :, 1:PAD], un.o[:, :, 0:STEPS],
                                        ALU.subtract).then_inc(s["k_oprev"], 1)

            def relus2(u):
                un = unit(u)
                dve.wait_ge(s["k_oprev"], u + 1)
                for c in range(CH):
                    nc.vector.tensor_scalar(un.ee[:, c, :], un.k_oprev[:, c, :], vec[:, XU, c:c + 1], 0.0,
                                            ALU.add, ALU.min).then_inc(s["relu_x"], 1)
                for c in range(CH):
                    nc.vector.tensor_scalar(un.aa[:, c, :], un.k_oprev[:, c, :], vec[:, XU, c:c + 1], 0.0,
                                            ALU.add, ALU.max).then_inc(s["relu_x"], 1)

            def scan_q(u):
                un = unit(u)
                dve.wait_ge(s["a2"], CH * (u + 1))
                dve.wait_ge(s["ek"], u + 1)
                nc.vector.tensor_tensor_scan(line(un.qst), line(un.a2), line(un.ek), 0.0, ALU.mult,
                                             ALU.add).then_inc(s["q_scan"], 1)

            def scan_p(u):
                un = unit(u)
                dve.wait_ge(s["a2"], CH * (u + 1))
                dve.wait_ge(s["k_oprev"], u + 1)
                dve.wait_ge(s["ekv"], u + 1)
                nc.vector.tensor_tensor_scan(line(un.pst), line(un.a2), line(un.ekv), 0.0, ALU.mult,
                                             ALU.add).then_inc(s["p_scan"], 1)

            def denominator2(u):
                un = unit(u)
                dve.wait_ge(s["aa"], u + 1)
                dve.wait_ge(s["q_scan"], u + 1)
                nc.vector.tensor_tensor(seg(un.den2), seg(un.aa), un.qst[:, :, 0:STEPS],
                                        ALU.mult).then_inc(s["aq"], 1)

                dve.wait_ge(s["aq"], u + 1)
                nc.vector.tensor_tensor(un.den2, un.den2, un.ee, ALU.add).then_inc(s["den2"], 1)

            def numerator2(u):
                un = unit(u)
                dve.wait_ge(s["p_scan"], u + 1)
                nc.vector.tensor_tensor(seg(un.num2), seg(un.aa), un.pst[:, :, 0:STEPS],
                                        ALU.mult).then_inc(s["ap"], 1)
                dve.wait_ge(s["ap"], u + 1)
                dve.wait_ge(s["ev"], u + 1)
                nc.vector.tensor_tensor(un.num2, un.num2, un.ev, ALU.add).then_inc(s["num2"], 1)

            def invert2(u):
                un = unit(u)
                dve.wait_ge(s["rd0"], u + 1)
                dve.wait_ge(s["ap"], u + 1)
                nc.vector.tensor_tensor(un.rdn, un.den2, un.rd0, ALU.mult).then_inc(s["gd"], 1)
                dve.wait_ge(s["gd"], u + 1)
                nc.vector.scalar_tensor_tensor(un.rdn, un.rdn, -2.0, un.rd0, ALU.add,
                                               ALU.mult).then_inc(s["rdn"], 1)

            def residual2(u):
                un = unit(u)
                dve.wait_ge(s["rdn"], u + 1)
                dve.wait_ge(s["num2"], u + 1)
                nc.vector.tensor_tensor(un.num2, un.num2, un.rdn, ALU.mult).then_inc(s["yn"], 1)
                dve.wait_ge(s["yn"], u + 1)
                nc.vector.scalar_tensor_tensor(seg(un.z[1]), seg(un.num2), -1.0, un.x1[:, :, 1:PAD],
                                               ALU.mult, ALU.add).then_inc(s_z[1], 1)

            wide = lambda t_: t_[:, :].unsqueeze(2).to_broadcast([P, TH, EXPERTS])

            def router_a(hf):
                logits = ps[:, 3, 0:TH * EXPERTS].rearrange("p (t e) -> p t e", t=TH)
                dve.wait_ge(s["logits"], hf + 1)
                nc.vector.tensor_reduce(top[:, :], logits, AX.X, ALU.max).then_inc(s["top"], 1)
                dve.wait_ge(s["top"], hf + 1)
                nc.vector.tensor_tensor(ex[:, :, :], logits, wide(top), ALU.subtract).then_inc(s["shifted"], 1)

            def router_b(hf):
                dve.wait_ge(s["ex"], hf + 1)
                nc.vector.tensor_reduce(zsum[:, :], ex[:, :, :], AX.X, ALU.add).then_inc(s["zsum"], 1)
                dve.wait_ge(s["zsum"], hf + 1)
                nc.vector.reciprocal(zsum[:, :], zsum[:, :]).then_inc(s["rz"], 1)
                dve.wait_ge(s["rz"], hf + 1)
                nc.vector.tensor_tensor(probs[:, :, :], ex[:, :, :], wide(zsum), ALU.mult).then_inc(s["probs"], 1)
                dve.wait_ge(s["probs"], hf + 1)
                for t in range(TH):
                    nc.vector.max(best[:, t, :], probs[:, t, :]).then_inc(s["best"], 1)
                for t in range(TH):
                    dve.wait_ge(s["best"], TH * hf + t + 1)
                    nc.vector.match_replace(marked[:, t, :], best[:, t, :], probs[:, t, :],
                                            -1.0).then_inc(s["marked"], 1)
                dve.wait_ge(s["marked"], TH * (hf + 1))
                nc.vector.scalar_tensor_tensor(probs[:, :, :], marked[:, :, :], 0.0, probs[:, :, :],
                                               ALU.is_lt, ALU.mult).then_inc(s["chosen"], 1)
                dve.wait_ge(s["chosen"], hf + 1)
                nc.vector.tensor_reduce(csum[:, :], probs[:, :, :], AX.X, ALU.add).then_inc(s["csum"], 1)
                dve.wait_ge(s["csum"], hf + 1)
                nc.vector.reciprocal(csum[:, :], csum[:, :]).then_inc(s["rcs"], 1)
                dve.wait_ge(s["rcs"], hf + 1)
                nc.vector.tensor_tensor(probs[:, :, :], probs[:, :, :], wide(csum), ALU.mult).then_inc(s["gate"], 1)

            def weigh(n, j):
                if isinstance(n, int):
                    dve.wait_ge(s_gates[j], 16 * HALVES)
                dve.wait_ge(s["silu"], n + 1)
                nc.vector.tensor_tensor(sg[j % 2][:, :], sg[j % 2][:, :], gates[:, 1, j, :],
                                        ALU.mult).then_inc(s["sw"], 1)

            def hidden(n, i):
                dve.wait_ge(s["sw"], n + 1)
                dve.wait_ge(s["u"], n + 1)
                nc.vector.tensor_tensor(h[i][:, :], ps[:, 5 + 2 * i, :], sg[i][:, :],
                                        ALU.mult).then_inc(s["h"], 1)

            def rest_h(n, i):
                dve.wait_ge(s["hh"], n + 1)
                need(dve, s["down"], n - 1)
                nc.vector.tensor_tensor(hl[i][:, :], h[i][:, :], hh[i][:, :].bitcast(f32),
                                        ALU.subtract).then_inc(s["hl"], 1)

            ZEROS = 3 + len(units)
            nc.vector.memset(avg[:, :], 1.0 / DIM).then_inc(s["consts"], 1)
            nc.vector.memset(eps[:, :], EPS).then_inc(s["zeros"], 1)
            nc.vector.memset(decay[:, :, :, :], 0.0).then_inc(s["zeros"], 1)
            for un in units:
                nc.vector.memset(un.x1[:, :, 0:1], FAR).then_inc(s["zeros"], 1)
            nc.vector.memset(zero[:, :].bitcast(f32), 0.0).then_inc(s["zeros"], 1)
            dve.wait_ge(s_vec, 16)
            v = lambda i: vec[:, i, :]
            nc.vector.tensor_tensor(kw[:, :], v(BK), v(U_), ALU.add).then_inc(s["zeros"], 1)
            nc.vector.tensor_scalar(w2n[:, :], v(W_), -2.0, None, ALU.mult).then_inc(s["consts"], 1)
            nc.vector.tensor_scalar(xun[:, :], v(XU), -1.0, None, ALU.mult).then_inc(s["consts"], 1)
            dve.wait_ge(s["zeros"], ZEROS + 1)
            nc.vector.tensor_tensor(wk[:, :], v(W_), kw[:, :], ALU.subtract).then_inc(s["consts"], 1)
            dve.wait_ge(s["consts"], 4)
            nc.vector.tensor_scalar(kw[:, :], wk[:, :], -1.0, None, ALU.mult).then_inc(s["consts"], 1)
            set_decay()
            diff(0)
            mix_kv(0)
            mix_r(0)
            diff(1)
            mix_kv(1)
            mix_r(1)
            scans1(0)
            invert1(0, 0)
            invert1(0, 1)
            scans1(1)
            times_r(0)
            invert1(1, 0)
            invert1(1, 1)
            residual1(0)
            weigh1(1)
            times_r(1)
            center(0, 0)
            mix_kv(2)
            residual1(1)
            center(0, 1)
            norm1(0)
            max_scan(0)
            step_of_o(0)
            against_o(0)
            norm1(1)
            max_scan(1)
            step_of_o(1)
            against_o(1)
            scan_q(0)
            denominator2(0)
            scan_p(0)
            scan_q(1)
            numerator2(0)
            invert2(0)
            denominator2(1)
            scan_p(1)
            residual2(0)
            mix_kv(3)
            center(1, 0)
            invert2(1)
            residual2(1)
            center(1, 1)
            norm2(0)
            relus1(2)
            norm2(1)
            rest_x2(0)
            router_a(0)
            rest_x2(1)
            relus1(3)
            router_b(0)
            scans1(2)
            scans1(3)
            invert1(2, 0)

            def step(n, i):
                hidden(n, i)
                rest_h(n, i)

            for n in range(TILES):
                step(n, n % 2)
                if n == 0:
                    invert1(2, 1)
                    weigh1(2)
                    times_r(2)
                if n == 1:
                    residual1(2)
                    invert1(3, 0)
                if n == 2:
                    center(0, 2)
                if n == 3:
                    invert1(3, 1)
                if n == 4:
                    weigh1(3)
                    times_r(3)
                if n == 5:
                    norm1(2)
                    residual1(3)
                    max_scan(2)
                    against_o_before(2)
                    center(0, 3)
                    relus2(2)
                    against_o(2)
                    step_of_o(2)
                    norm1(3)
                if n == 6:
                    max_scan(3)
                    scan_q(2)
                    against_o_before(3)
                if n == 7:
                    relus2(3)
                if n == 8:
                    against_o(3)
                if n == 9:
                    step_of_o(3)
                if n == 10:
                    denominator2(2)
                    scan_p(2)
                    numerator2(2)
                if n == 11:
                    invert2(2)
                    scan_p(3)
                    residual2(2)
                if n == 12:
                    scan_q(3)
                    denominator2(3)
                if n == 13:
                    center(1, 2)
                if n == 14:
                    numerator2(3)
                if n == 15:
                    invert2(3)
                    residual2(3)
                if n == 16:
                    center(1, 3)
                if n == 18:
                    norm2(2)
                    norm2(3)
                if n == 19:
                    router_a(1)
                if n == 20:
                    router_b(1)
                if n == 21:
                    rest_x2(2)
                    rest_x2(3)

            def residual3(k):
                at, w = slice(*parts3[k]), parts3[k][1] - parts3[k][0]
                a, hf = parts3[k][0] % HT, parts3[k][0] // HT
                dve.wait_ge(s["sums"], hf + 1)
                nc.vector.tensor_tensor(z3[:, :, at], ps[:, 2 * hf:2 * hf + 2, a:a + w], x2[:, :, at],
                                        ALU.add).then_inc(s["z3"], 1)

            def center3(k):
                at, w = slice(*parts3[k]), parts3[k][1] - parts3[k][0]
                dve.wait_ge(s["mean3"], k + 1)
                nc.vector.tensor_tensor(z3[:, :, at], z3[:, :, at],
                                        ps[:, mean3_bank[k], 0:w].unsqueeze(1).to_broadcast([P, CH, w]),
                                        ALU.subtract).then_inc(s["cen3"], 1)

            def norm3(k):
                at, w = slice(*parts3[k]), parts3[k][1] - parts3[k][0]
                dve.wait_ge(s["r0sq3"], k + 1)
                nc.vector.scalar_tensor_tensor(vr3[:, at], ps[:, var3_bank[k], 0:w], EPS, vr3[:, at],
                                               ALU.add, ALU.mult).then_inc(s["vr3"], 1)
                dve.wait_ge(s["vr3"], k + 1)
                nc.vector.scalar_tensor_tensor(vr3[:, at], vr3[:, at], -3.0, r03[:, at], ALU.add,
                                               ALU.mult).then_inc(s["rn3"], 1)
                dve.wait_ge(s["rn3"], k + 1)
                nc.vector.scalar_tensor_tensor(z3[:, :, at], z3[:, :, at], -0.5,
                                               vr3[:, at].unsqueeze(1).to_broadcast([P, CH, w]),
                                               ALU.mult, ALU.mult).then_inc(s["y3"], 1)

            for j in range(GROUPS):
                weigh(TILES + j, j)
                step(TILES + j, j % 2)
                if j == 2:
                    residual3(0)
                if j == 4:
                    center3(0)
                if j == 7:
                    norm3(0)
            with dve.Fori(TILES // GROUPS + 1, STEPS_ALL // GROUPS) as q:
                for j in range(GROUPS):
                    weigh(GROUPS * q + j, j)
                    step(GROUPS * q + j, j % 2)
            for f in (residual3, center3, norm3):
                for k in (1, 2):
                    f(k)

        @block.tensor
        def _(pe):
            mm = nc.tensor.matmul

            def project(b, which, src):
                for mo in range(CH):
                    for k in range(CH):
                        last = mm(pc(b)[:, mo, :], wp[:, which, k, mo * P:(mo + 1) * P], src(k),
                                  start=(k == 0), stop=(k == CH - 1))
                return last

            def project_k(u):
                if u >= 2:
                    pe.wait_ge(s["y1"], CH * (u - 1))
                pe.wait_ge(s["kvmixed"], 2 * CH * u + CH)
                project(bank(u, "k"), K_, lambda k: kvmix(u, 0)[:, k, :]).then_inc(s["k_proj"], 1)

            def project_v(u):
                if u == 0:
                    pe.wait_ge(s_wp[1], 16)
                if u >= 2:
                    pe.wait_ge(s_z[0], CH * (u - 1))
                pe.wait_ge(s["kvmixed"], 2 * CH * (u + 1))
                project(bank(u, "v"), V_, lambda k: kvmix(u, 1)[:, k, :]).then_inc(s["v_proj"], 1)

            def project_r(u):
                if u >= 2:
                    pe.wait_ge(s["kept_k"], CH * (u - 1))
                pe.wait_ge(s["silu_r"], u // 2 + 1)
                seqs = slice(u * UNIT_SEQS, (u + 1) * UNIT_SEQS)
                project(bank(u, "r"), R_, lambda k: rmix[:, k, seqs, :]).then_inc(s["r_proj"], 1)

            def project_out(u):
                pe.wait_ge(s["y1"], CH * (u + 1))
                project(bank(u, "o"), O_, lambda k: unit(u).num1[:, k, :]).then_inc(s["o_proj"], 1)

            def mean(n, u):
                pe.wait_ge(s_z[n], (CH if n == 0 else 1) * (u + 1))
                for k in range(CH):
                    last = mm(ps[:, bank(u, f"ln{n}"), 0:UT], avg[:, :], unit(u).z[n][:, k, :],
                              start=(k == 0), stop=(k == CH - 1))
                last.then_inc(s_mean[n], 1)

            def variance(n, u):
                pe.wait_ge(s_sq[n], u + 1)
                for k in range(CH):
                    last = mm(ps[:, bank(u, f"ln{n}"), UT:2 * UT], avg[:, :], unit(u).sq[n][:, k, :],
                              start=(k == 0), stop=(k == CH - 1))
                last.then_inc(s_var[n], 1)

            def route(hf):
                if hf == 0:
                    pe.wait_ge(s_small, 16 * 2)
                    pe.wait_ge(s["kept_v"], CH)
                for t in range(TH):
                    if t % (UT // P) == 0:
                        pe.wait_ge(s["x2"], 2 * (hf + 1) if hf else t // (UT // P) + 1)
                    a = (TH * hf + t) * P
                    for k in range(CH):
                        last = mm(ps[:, 3, t * EXPERTS:(t + 1) * EXPERTS], x2[:, k, a:a + P],
                                  rw[:, k, :], start=(k == 0), stop=(k == CH - 1))
                last.then_inc(s["logits"], 1)

            def turn_gates(hf):
                if hf == 0:
                    pe.wait_ge(s["kept_r"], CH)
                pe.wait_ge(s["gate"], hf + 1)
                for t in range(TH):
                    last = nc.tensor.transpose(ps[0:EXPERTS, 2, t * P:(t + 1) * P],
                                               probs[:, t, :], ident[:, :])
                last.then_inc(s["gateT_ps"], 1)

            def up(which, n, j, hf):
                i, w_ = j % 2, j % SLOTS
                if which == 0:
                    pe.wait_ge(s["w_hi"], n + 1)
                need_ = s["silu" if which == 0 else "h"]
                if not isinstance(n, int) or n >= 2:
                    pe.wait_ge(need_, n - 1)
                parts = [(k, whi, x_) for k in range(CH) for x_ in (x2h, x2l)]
                parts += [(k, wlo, x2h) for k in range(CH)]
                for m, (k, part, x_) in enumerate(parts):
                    a = which * DIM + k * P
                    if part is wlo and which == 0:
                        pe.wait_ge(s["w_lo"], n + 1)
                    last = mm(ps[:, 4 + 2 * i + which, :], part[w_][:, a:a + P],
                              x_[:, k, hf * HT:(hf + 1) * HT], start=(m == 0), stop=(m == len(parts) - 1))
                last.then_inc(s["g" if which == 0 else "u"], 1)

            def down(n, j, hf, last_one=False):
                i, w_ = j % 2, j % SLOTS
                pe.wait_ge(s["hh"], n + 1)
                pe.wait_ge(s["hl"], n + 1)
                for mo in range(CH):
                    a = 2 * DIM + mo * P
                    for w__, h_ in ((whi, hh), (whi, hl), (wlo, hh)):
                        last = mm(ps[:, 2 * hf + mo, :], w__[w_][:, a:a + P], h_[i][:, :],
                                  start=False, stop=last_one and w__ is wlo)
                last.then_inc(s["sums" if last_one else "down"], 1)

            def sums(hf, **flag):
                for mo in range(CH):
                    last = mm(ps[:, 2 * hf + mo, :], zero[:, :], x2h[:, 0, hf * HT:(hf + 1) * HT], **flag)
                return last

            pe.wait_ge(s_wp[0], 16)
            pe.wait_ge(s["consts"], 1)
            project_k(0)
            project_v(0)
            project_k(1)
            project_r(0)
            project_v(1)
            project_r(1)
            project_out(0)
            mean(0, 0)
            project_out(1)
            variance(0, 0)
            mean(0, 1)
            variance(0, 1)
            project_k(2)
            project_r(2)
            project_v(2)
            mean(1, 0)
            project_k(3)
            variance(1, 0)
            mean(1, 1)
            project_r(3)
            variance(1, 1)
            project_v(3)
            route(0)

            def step(n, j, hf):
                up(0, n, j, hf)
                down(n - 2, j - 2, hf)
                up(1, n, j, hf)

            pe.wait_ge(s["x2h"], 2)
            pe.wait_ge(s["x2l"], 2)
            up(0, 0, 0, 0)
            up(1, 0, 0, 0)
            pe.wait_ge(s["zeros"], 5)
            sums(0, start=True, stop=False)
            turn_gates(0)
            pe.wait_ge(s["kept_r"], 2 * CH)
            pe.wait_ge(s["kept_v"], 2 * CH)
            up(0, 1, 1, 0)
            up(1, 1, 1, 0)
            for n in range(2, TILES):
                step(n, n, 0)
                if n == 2:
                    project_out(2)
                if n == 3:
                    mean(0, 2)
                if n == 5:
                    variance(0, 2)
                    project_out(3)
                if n == 6:
                    mean(0, 3)
                    variance(0, 3)
                if n == 13:
                    mean(1, 2)
                if n == 17:
                    mean(1, 3)
                if n == 18:
                    variance(1, 2)
                    variance(1, 3)
                if n == 20:
                    route(1)
                if n == 22:
                    turn_gates(1)
            pe.wait_ge(s["gateT"], 2)

            pe.wait_ge(s["x2h"], 4)
            pe.wait_ge(s["x2l"], 4)
            sums(1, start=True, stop=False)
            for j in range(2):
                up(0, TILES + j, j, 1)
                down(TILES - 2 + j, TILES - 2 + j, 0)
                up(1, TILES + j, j, 1)
            sums(0, start=False, stop=True).then_inc(s["sums"], 1)
            def average3(k, of, bank_, sm):
                (a, b) = parts3[k]
                for c in range(CH):
                    last = mm(ps[:, bank_[k], 0:b - a], avg[:, :], of[:, c, a:b],
                              start=(c == 0), stop=(c == CH - 1))
                last.then_inc(sm, 1)

            def mean3(k):
                pe.wait_ge(s["z3"], k + 1)
                average3(k, z3, mean3_bank, s["mean3"])

            def variance3(k):
                pe.wait_ge(s["sq3"], k + 1)
                average3(k, sq3, var3_bank, s["var3"])

            for j in range(2, GROUPS):
                step(TILES + j, j, 1)
                if j == 4:
                    mean3(0)
                if j == 6:
                    variance3(0)
            with pe.Fori(TILES // GROUPS + 1, STEPS_ALL // GROUPS) as q:
                for j in range(GROUPS):
                    step(GROUPS * q + j, GROUPS + j, 1)
            down(STEPS_ALL - 2, STEPS_ALL - 2, 1)
            down(STEPS_ALL - 1, STEPS_ALL - 1, 1, last_one=True)
            for f in (mean3, variance3):
                for k in (1, 2):
                    f(k)


def kernel(**inputs):
    import numpy as np
    import concourse.bacc as bacc
    from concourse.bass_utils import run_bass_kernel_spmd as run

    a = {n: np.asarray(v) for n, v in inputs.items()}
    at = {n[len("L0_attn_"):]: v for n, v in a.items() if n.startswith("L0_attn_")}

    def channels(t):
        return t.reshape(SEQS, STEPS, CH, P).transpose(3, 2, 0, 1)

    def rows(w):
        return w.T.reshape(CH, P, -1).transpose(1, 0, 2)

    vectors = [at["bk"], at["bv"], at["br"], at["bo"], at["tmk"], at["tmv"], at["tmr"], at["u"],
               at["w"], a["L0_xattn_w"], a["L0_xattn_u"]]

    def up_rows(w):
        w = w.reshape(GROUPS, EG, CH, P, INNER // IG, IG).transpose(4, 0, 3, 2, 1, 5)
        return w.reshape(TILES, P, CH * P)

    down_rows = a["L0_ffn_w_down"].reshape(GROUPS, EG, INNER // IG, IG, DIM).transpose(
        2, 0, 1, 3, 4)
    arrays = {
        "xT": channels(a["x"]),
        "ctxT": channels(a["ctx_2048"]),
        "wproj": np.stack([rows(at[n]) for n in ("Wk", "Wv", "Wr", "Wo")], axis=1),
        "vecs": np.stack([v.reshape(CH, P).T for v in vectors], axis=1),
        "routerT": rows(a["L0_ffn_router_w"]),
        "experts": np.concatenate([up_rows(a["L0_ffn_w_gate"]), up_rows(a["L0_ffn_w_up"]),
                                   down_rows.reshape(TILES, P, DIM)], axis=2),
        "eye": np.eye(P, dtype=np.float32),
    }
    arrays = {n: np.ascontiguousarray(v) for n, v in arrays.items()}
    nc = bacc.Bacc("TRN2", target_bir_lowering=False, num_devices=1)
    args = [nc.dram_tensor(f"in_{n}", v.shape, mybir.dt.from_np(v.dtype), kind="ExternalInput").ap()
            for n, v in arrays.items()]
    out = nc.dram_tensor("out", (P, CH, TOK), mybir.dt.float32, kind="ExternalOutput").ap()
    build(nc, *args, out)
    r = run(nc, [{f"in_{n}": v for n, v in arrays.items()}], core_ids=[0])
    y = np.asarray(r.results[0]["out"])
    return y.transpose(2, 1, 0).reshape(SEQS, STEPS, DIM)
```
